# Optimizing a Trainium2 kernel written in Bass

```python
import numpy as np
import jax
import jax.numpy as jnp

def _softmax(x, axis=-1):
    return jax.nn.softmax(x, axis=axis)

def _gelu(x):
    return jax.nn.gelu(x, approximate=True)

def _silu(x):
    return jax.nn.silu(x)

def _sigmoid(x):
    return jax.nn.sigmoid(x)

def _layernorm(x, axis=-1, eps=1e-05):
    m = jnp.mean(x, axis=axis, keepdims=True)
    v = jnp.var(x, axis=axis, keepdims=True)
    return (x - m) / jnp.sqrt(v + eps)

def _scatter_add(tgt, idx, src, axis=0):
    return tgt.at[idx].add(src)

def _segment_sum(src, seg, n):
    return jax.ops.segment_sum(src, seg, n)
kernel_name = 'mk_seq_postln_d1_jaxref_r8_8e675a'

def setup_inputs(seed: int=0):
    np.random.seed(seed)
    _w = jnp.asarray

    def _L0_attn_setup():
        import jax, jax.numpy as jnp
        import numpy as np
        D_MODEL = 256
        N_HEADS = 16
        D_K = D_MODEL // N_HEADS
        EPS = 1e-06
        key = jax.random.key(seed)
        ks = jax.random.split(key, 9)
        s = 1.0 / np.sqrt(D_MODEL)
        return {'x': jax.random.normal(ks[0], (4, 512, D_MODEL), dtype=jnp.float32), 'Wq': jax.random.normal(ks[1], (D_MODEL, D_MODEL), dtype=jnp.float32) * s, 'bq': jnp.zeros((D_MODEL,), dtype=jnp.float32), 'Wk': jax.random.normal(ks[2], (D_MODEL, D_MODEL), dtype=jnp.float32) * s, 'bk': jnp.zeros((D_MODEL,), dtype=jnp.float32), 'Wv': jax.random.normal(ks[3], (D_MODEL, D_MODEL), dtype=jnp.float32) * s, 'bv': jnp.zeros((D_MODEL,), dtype=jnp.float32), 'Wo': jax.random.normal(ks[4], (D_MODEL, D_MODEL), dtype=jnp.float32) * s, 'bo': jnp.zeros((D_MODEL,), dtype=jnp.float32)}
    _L0_attn_in = _L0_attn_setup()

    def _L0_ffn_setup():
        import jax, jax.numpy as jnp
        import numpy as np
        H = 256
        E = 8
        TOPK = 2
        I_MOE = 128
        I_SH = 512

        def _silu_and_mul(gu):
            g, u = jnp.split(gu, 2, axis=-1)
            return jax.nn.silu(g) * u
        key = jax.random.key(seed)
        ks = jax.random.split(key, 6)
        s = lambda *sh: 1.0 / np.sqrt(sh[-2])
        hidden_states = jax.random.normal(ks[0], (2, 128, H), dtype=jnp.float32)
        w_gate = jax.random.normal(ks[1], (H, E), dtype=jnp.float32) * (1.0 / np.sqrt(H))
        w_gate_up = jax.random.normal(ks[2], (E, H, 2 * I_MOE), dtype=jnp.float32) * (1.0 / np.sqrt(H))
        w_down = jax.random.normal(ks[3], (E, I_MOE, H), dtype=jnp.float32) * (1.0 / np.sqrt(I_MOE))
        w_sh_gate_up = jax.random.normal(ks[4], (H, 2 * I_SH), dtype=jnp.float32) * (1.0 / np.sqrt(H))
        w_sh_down = jax.random.normal(ks[5], (I_SH, H), dtype=jnp.float32) * (1.0 / np.sqrt(I_SH))
        return {'hidden_states': hidden_states, 'w_gate': w_gate, 'w_gate_up': w_gate_up, 'w_down': w_down, 'w_sh_gate_up': w_sh_gate_up, 'w_sh_down': w_sh_down}
    _L0_ffn_in = _L0_ffn_setup()
    _d = {'L0_attn_x': _L0_attn_in['x'], 'L0_attn_Wq': _L0_attn_in['Wq'], 'L0_attn_bq': _L0_attn_in['bq'], 'L0_attn_Wk': _L0_attn_in['Wk'], 'L0_attn_bk': _L0_attn_in['bk'], 'L0_attn_Wv': _L0_attn_in['Wv'], 'L0_attn_bv': _L0_attn_in['bv'], 'L0_attn_Wo': _L0_attn_in['Wo'], 'L0_attn_bo': _L0_attn_in['bo'], 'L0_ffn_w_gate': _L0_ffn_in['w_gate'], 'L0_ffn_w_gate_up': _L0_ffn_in['w_gate_up'], 'L0_ffn_w_down': _L0_ffn_in['w_down'], 'L0_ffn_w_sh_gate_up': _L0_ffn_in['w_sh_gate_up'], 'L0_ffn_w_sh_down': _L0_ffn_in['w_sh_down']}
    _x0 = _d['L0_attn_x']
    _d['L0_attn_x'] = jax.random.normal(jax.random.fold_in(jax.random.key(seed), 1), (4, 512, 256), dtype=_x0.dtype)
    del _x0
    return _d

def reference(L0_attn_x, L0_attn_Wq, L0_attn_bq, L0_attn_Wk, L0_attn_bk, L0_attn_Wv, L0_attn_bv, L0_attn_Wo, L0_attn_bo, L0_ffn_w_gate, L0_ffn_w_gate_up, L0_ffn_w_down, L0_ffn_w_sh_gate_up, L0_ffn_w_sh_down):

    def _L0_attn_ref(x, Wq, bq, Wk, bk, Wv, bv, Wo, bo):
        import jax, jax.numpy as jnp
        import numpy as np
        D_MODEL = 256
        N_HEADS = 16
        D_K = D_MODEL // N_HEADS
        EPS = 1e-06
        b, n, _ = x.shape
        h, d = (N_HEADS, D_K)

        def proj(W, bias):
            y = jnp.einsum('bnm,dm->bnd', x, W) + bias
            return y.reshape(b, n, h, d).transpose(0, 2, 1, 3)
        Q = jax.nn.relu(proj(Wq, bq))
        K = jax.nn.relu(proj(Wk, bk))
        V = proj(Wv, bv)
        pos = jnp.arange(n, dtype=x.dtype)
        decay = jnp.exp(-pos / n)[None, None, :, None]
        Q = Q * decay
        K = K * decay
        KV = jnp.einsum('bhnd,bhne->bhde', K, V)
        Ksum = K.sum(axis=2)
        Z = 1.0 / (jnp.einsum('bhnd,bhd->bhn', Q, Ksum)[..., None] + EPS)
        out = jnp.einsum('bhnd,bhde->bhne', Q, KV) * Z
        out = out.transpose(0, 2, 1, 3).reshape(b, n, h * d)
        return jnp.einsum('bnm,dm->bnd', out, Wo) + bo

    def _L0_ffn_ref(hidden_states, w_gate, w_gate_up, w_down, w_sh_gate_up, w_sh_down):
        import jax, jax.numpy as jnp
        import numpy as np
        H = 256
        E = 8
        TOPK = 2
        I_MOE = 128
        I_SH = 512

        def _silu_and_mul(gu):
            g, u = jnp.split(gu, 2, axis=-1)
            return jax.nn.silu(g) * u
        orig_shape = hidden_states.shape
        x = hidden_states.reshape(-1, orig_shape[-1])
        router_logits = x @ w_gate
        probs = jax.nn.softmax(router_logits, axis=-1)
        topk_w, topk_ids = jax.lax.top_k(probs, TOPK)
        topk_w = topk_w / jnp.sum(topk_w, axis=-1, keepdims=True)
        combine = jnp.sum(topk_w[..., None] * jax.nn.one_hot(topk_ids, E, dtype=x.dtype), axis=1)
        gu = jnp.einsum('th,ehf->etf', x, w_gate_up)
        act = _silu_and_mul(gu)
        eo = jnp.einsum('eti,eih->eth', act, w_down)
        routed = jnp.einsum('te,eth->th', combine, eo)
        shared = _silu_and_mul(x @ w_sh_gate_up) @ w_sh_down
        return (routed + shared).reshape(orig_shape)
    x = L0_attn_x
    x = _layernorm(x + _L0_attn_ref(x, L0_attn_Wq, L0_attn_bq, L0_attn_Wk, L0_attn_bk, L0_attn_Wv, L0_attn_bv, L0_attn_Wo, L0_attn_bo), axis=-1)
    x = _layernorm(x + _L0_ffn_ref(x, L0_ffn_w_gate, L0_ffn_w_gate_up, L0_ffn_w_down, L0_ffn_w_sh_gate_up, L0_ffn_w_sh_down), axis=-1)
    return x

_drawn_inputs = setup_inputs


def setup_inputs(seed=0):
    import zlib

    import numpy as np

    out = dict(_drawn_inputs(seed))
    spreads = {'L0_attn_bq': (0.0, 0.339),
     'L0_attn_bk': (0.0, 0.394),
     'L0_attn_bv': (0.0, 0.1),
     'L0_attn_bo': (0.0, 0.1)}
    factors = {}
    for name, (base, spread) in spreads.items():
        noise = np.random.default_rng([zlib.crc32(name.encode()), seed]).standard_normal(out[name].shape)
        drawn = base * np.exp(spread * noise) if base else spread * noise
        out[name] = jnp.asarray(drawn.astype(out[name].dtype))
    for name, factor in factors.items():
        out[name] = (out[name] * factor).astype(out[name].dtype)
    return out
```

```python
from contextlib import ExitStack

import numpy as np

import concourse.bass as bass
from concourse import mybir

F32 = mybir.dt.float32
F32R = mybir.dt.float32r
BF16 = mybir.dt.bfloat16
I32 = mybir.dt.int32
U32 = mybir.dt.uint32
ALU = mybir.AluOpType
ACT = mybir.ActivationFunctionType
AX = mybir.AxisListType

P = 128
NB, SEQ, D = 4, 512, 256
KD = D // P
NH, DH = 16, 16
HB = P // DH
NE, TOPK, IM, IS = 8, 2, 128, 512
CS = IS // P
TB = SEQ // P
T = NB * TB
TOK = NB * SEQ
NT = -(-((TOK * TOPK + NE * (P - 1)) // P) // 4) * 4
NSLOT = NT * P
EPS_ATT, EPS_LN = 1e-6, 1e-5
AW = KD * 2 * D + KD * D + KD * D
WKV, WQ, WO = 0, KD * 2 * D, KD * 2 * D + KD * D
SH_GU = 0
SH_DN = SH_GU + KD * 2 * IS
EX = SH_DN + CS * D
EX_W = KD * 2 * IM + D
FW = EX + NE * EX_W
CHUNK = 512
NCH = FW // CHUNK
RING = 4
WORDS = NT // RING + 1
WORD_TILES = RING + 2
NTW = (WORDS + 1) * RING
E_BITS = (NE - 1).bit_length()
C_ID, C_BLK = 0, P
C_HEAD = C_BLK + P
C_DEC = C_HEAD + HB
C_EPS = C_DEC + TB
C_IOTA = C_EPS + TB
C_TRI = C_IOTA + NE
C_TILE = C_TRI + P
NC_ = C_TILE + NTW
RSQRT_MAGIC = 0x5F3759DF


def build(nc, xT, x, watt, batt, bq, wffn, wgate, consts, out):
    x_scat = nc.dram_tensor("x_slots", [NSLOT, D], F32).ap()
    y_scat = nc.dram_tensor("y_slots", [NSLOT, D], F32).ap()
    ctx = ExitStack()
    with ctx:
        def sb(name, shape, dt=F32):
            return ctx.enter_context(nc.sbuf_tensor(name, shape, dt))

        def sem(name):
            return ctx.enter_context(nc.semaphore(name))

        cst = sb("cst", [P, NC_])
        tri = sb("tri", [P, P], BF16)
        ones = sb("ones", [P, P], BF16)
        one_f = sb("one_f", [33, P], F32R)
        b_row = sb("b_row", [33, 3 * D], F32R)
        bq_sb = sb("bq_sb", [P, KD])
        wg_sb = sb("wg_sb", [P, KD, NE])
        wa_hi = sb("wa_hi", [P, AW], F32R)
        wa_lo = sb("wa_lo", [P, AW], F32R)
        wf_hi = sb("wf_hi", [P, FW], F32R)
        wf_lo = sb("wf_lo", [P, FW], F32R)
        stage = sb("stage", [P, 2, CHUNK])
        xt_raw = sb("xt_raw", [P, 2, KD, SEQ])
        xt_hi = sb("xt_hi", [P, 2, KD, SEQ], F32R)
        xt_lo = sb("xt_lo", [P, 2, KD, SEQ], F32R)
        x1 = sb("x1", [P, T, D])
        wa_raw = x1[:, T // 2:, :].rearrange("p t d -> p (t d)")
        k_sb = sb("k_sb", [P, TB, D])
        v_sb = sb("v_sb", [P, TB, KD, P + 1])
        q_t = sb("q_t", [P, KD, SEQ])
        kvm = sb("kvm", [P, KD, P + HB])
        z = sb("z", [P, 2, KD, HB])
        o_sb = sb("o_sb", [P, TB, D])
        ot_hi = sb("ot_hi", [P, KD, SEQ], F32R)
        ot_lo = sb("ot_lo", [P, KD, SEQ], F32R)
        x1_t = sb("x1_t", [P, KD, SEQ])
        x1t_hi = sb("x1t_hi", [P, NB, KD, SEQ], F32R)
        x1t_lo = sb("x1t_lo", [P, NB, KD, SEQ], F32R)
        stat = sb("stat", [P, TB, 6])
        mv = sb("mv", [P, TB, 2])
        nw = sb("nw", [P, 5, TB])
        nwi = sb("nwi", [P, TB], I32)
        logit = sb("logit", [P, T, NE])
        top_v = sb("top_v", [P, T, 8])
        top_i = sb("top_i", [P, T, 8], U32)
        ix_f = sb("ix_f", [P, T, TOPK])
        hot = sb("hot", [P, TOPK, T * NE])
        hot_m = sb("hot_m", [P, T * NE], BF16)
        pos = sb("pos", [P, T * NE])
        slot_f = sb("slot_f", [P, TOPK, T])
        slot = sb("slot", [P, TOPK, T], U32)
        w_top = sb("w_top", [P, TOPK, T])
        wtmp = sb("wtmp", [P, 3, T])
        cnt = sb("cnt", [P, 6, NE])
        cnt_i = sb("cnt_i", [P, 2, NE], I32)
        te_c = sb("te_c", [1, NTW, NE])
        te_f = sb("te_f", [1, NTW])
        te_w = sb("te_w", [1, WORDS])
        te_i = sb("te_i", [1, WORDS], I32)
        b_raw = k_sb[0:33, 0:3, :].rearrange("p a d -> p (a d)")
        stage_zero = x1t_hi[:, NB - 1, :, :].rearrange("p k n -> p (k n)").bitcast(F32)
        sg, hf = xt_raw[:, 0], xt_raw[:, 1]
        hh_hi = xt_hi[:, :, :, :].rearrange("p a k n -> p (a k) n")
        hh_lo = xt_lo[:, :, :, :].rearrange("p a k n -> p (a k) n")
        xg = o_sb
        ey = x1_t[:, :, :].rearrange("p k (a n) -> p (k a) n", a=2)
        xe_hi, xe_lo = (o[:, 0, :].rearrange("p (a k n) -> p a k n", a=2, k=KD) for o in (ot_hi, ot_lo))
        he_hi, he_lo = (o[:, 1, 0:2 * IM].rearrange("p (a n) -> p a n", a=2) for o in (ot_hi, ot_lo))
        eg = q_t[:, 0, 0:2 * IM].rearrange("p (a n) -> p a n", a=2)
        eh = q_t[:, 1, 0:2 * IM].rearrange("p (a n) -> p a n", a=2)
        g_1 = k_sb
        g_2 = v_sb[:, :, :, :].rearrange("p t k n -> p (t k n)")[:, 0:TB * D].rearrange(
            "p (t d) -> p t d", t=TB)

        ident = cst[:, C_ID:C_ID + P]
        blk = cst[:, C_BLK:C_BLK + P]
        headm = cst[:, C_HEAD:C_HEAD + HB]

        bank = [ctx.enter_context(nc.psum_tensor(f"bank{i}", [P, 512], F32)) for i in range(8)]

        names = """b_cleared cst_in bias_in small_in watt_in0 watt_in1 watt_in2 res_in0 res_in1 res_in2 res_in3
            xt_in0 xt_in1 stage_in0 stage_in1 zero_in
            bf_ready bias_ready ones_ready kvw_split qw_split ow_split wf_split wf_staged_free
            xhi_ready xlo_ready kv_mm kv_out q_mm q_out kvp_mm kvm_out num_mm o_out ot_mm ot_hi_out ot_lo_out
            y_mm r_out x1_out x1t_mm x1f_out x1hi_out x1lo_out lg_mm lg_out
            hot_out rank_mm slots_out exp_in exp_out te_out scattered0 scattered1 scattered2 scattered3
            sgu_mm sg_out sh_out shh_out shl_out sdn_mm sres_out
            xt_e_mm xe_hi_out xe_lo_out egu_mm eg_out eh_out eht_mm he_hi_out he_lo_out ey_mm ey_out
            gath0 gath1 gath2 gath3 acc_out ln_out fin_out stored
            dve_chain pool_chain act_chain tail_norm""".split()
        S = {n: sem(n) for n in names}
        xg_in = [sem(f"xg_in{u}") for u in range(RING)]
        ey_st = [sem(f"ey_st{u}") for u in range(RING)]
        gath = [S[f"gath{u}"] for u in range(TB)]
        xt_in = [S["xt_in0"], S["xt_in1"]]
        stage_in = [S["stage_in0"], S["stage_in1"]]

        block = ctx.enter_context(nc.Block())

        @block.sync
        def _(sp):
            def load_xt(b):
                sp.dma_start(xt_raw[:, b % 2], xT[b].rearrange("p (k n) -> p k n", k=KD)).then_inc(xt_in[b % 2], 16)

            def load_res(b):
                sp.dma_start(x1[:, b * TB:(b + 1) * TB, :], x[b].rearrange("(t p) d -> p t d", p=P)
                             ).then_inc(S[f"res_in{b}"], 16)

            load_xt(0)
            sp.dma_start(wa_raw[:, WKV:WQ], watt[:, WKV:WQ]).then_inc(S["watt_in0"], 16)
            sp.dma_start(wa_raw[:, WQ:WO], watt[:, WQ:WO]).then_inc(S["watt_in1"], 16)
            load_xt(1)
            sp.dma_start(wa_raw[:, WO:AW], watt[:, WO:AW]).then_inc(S["watt_in2"], 16)
            load_res(0)
            load_res(1)

            def load_chunk(i):
                if i >= 2:
                    sp.wait_ge(S["wf_split"], 2 * (i - 1))
                sp.dma_start(stage[:, i % 2, :], wffn[:, i * CHUNK:(i + 1) * CHUNK]).then_inc(stage_in[i % 2], 16)

            for i in range(NCH):
                if i == 6:
                    sp.wait_ge(S["ow_split"], 2)
                    load_res(2)
                    load_res(3)
                if i in (5, 8):
                    b = 2 if i == 5 else 3
                    sp.wait_ge(S["xhi_ready"], b - 1)
                    sp.wait_ge(S["xlo_ready"], b - 1)
                    load_xt(b)
                load_chunk(i)

            for b in range(NB):
                sp.wait_ge(S[f"scattered{b}"], 16 * TOPK * TB)

            def load_tile(j, u, first=False):
                if not first:
                    sp.wait_ge(S["xt_e_mm"], j - RING + 1)
                sp.dma_start(xg[:, u, :], x_scat[bass.ds(j * P, P), :]).then_inc(xg_in[u], 16)

            def store_tile(j, u):
                sp.wait_ge(S["ey_out"], j + 1)
                sp.dma_start(y_scat[bass.ds(j * P, P), :], ey[:, u, :]).then_inc(ey_st[u], 16)

            for u in range(RING):
                load_tile(u, u, first=True)
            LAG = 3
            for u in range(LAG):
                load_tile(RING + u, u)
            with sp.Fori(0, NT // RING - 2) as i:
                for v in range(RING):
                    load_tile(i * RING + (RING + LAG + v), (LAG + v) % RING)
                    store_tile(i * RING + v, v)
            load_tile(NT - 1, RING - 1)
            for j in range(NT - 2 * RING, NT):
                store_tile(j, j % RING)

            for b in range(NB):
                sp.wait_ge(S["fin_out"], TB * (b + 1))
                sp.dma_start(out[b].rearrange("(t p) d -> p t d", p=P), x1[:, b * TB:(b + 1) * TB, :]
                             ).then_inc(S["stored"], 16)
            sp.wait_ge(S["stored"], 16 * NB)
            for u in range(RING):
                sp.wait_ge(ey_st[u], 16 * (NT // RING))

        @block.tensor
        def _(pe):
            mm = nc.tensor.matmul

            def split3(o, w_hi, w_lo, m_hi, m_lo, start, stop):
                mm(o, w_hi, m_hi, start=start, stop=False)
                mm(o, w_hi, m_lo, start=False, stop=False)
                return mm(o, w_lo, m_hi, start=False, stop=stop)

            def proj_kv(b, t):
                i = b * TB + t
                if t == 0:
                    pe.wait_ge(S["xhi_ready"], b + 1)
                    pe.wait_ge(S["xlo_ready"], b + 1)
                if i >= 2:
                    pe.wait_ge(S["kv_out"], i - 1)
                o = bank[t % 2][:, :]
                mm(o, one_f[:, :], b_row[:, 0:2 * D], start=True, stop=False)
                for k in range(KD):
                    c = slice(t * P, (t + 1) * P)
                    w = slice(WKV + k * 2 * D, WKV + (k + 1) * 2 * D)
                    last = split3(o, xt_hi[:, b % 2, k, c], xt_lo[:, b % 2, k, c], wa_hi[:, w], wa_lo[:, w],
                                  False, k == KD - 1)
                last.then_inc(S["kv_mm"], 1)

            def proj_q(b):
                if b == 0:
                    pe.wait_ge(S["qw_split"], 2)
                for m in range(KD):
                    if b >= 1:
                        pe.wait_ge(S["q_out"], KD * (b - 1) + m + 1)
                    if b >= 2:
                        pe.wait_ge(S["x1f_out"], KD * (b - 2) + m + 1)
                    o = bank[2 + m][:, :]
                    for k in range(KD):
                        w = slice(WQ + k * D + m * P, WQ + k * D + (m + 1) * P)
                        last = split3(o, wa_hi[:, w], wa_lo[:, w], xt_hi[:, b % 2, k, :], xt_lo[:, b % 2, k, :],
                                      k == 0, k == KD - 1)
                    last.then_inc(S["q_mm"], 1)

            def k_t_v(b):
                pe.wait_ge(S["kv_out"], TB * (b + 1))
                if b >= 1:
                    pe.wait_ge(S["ot_hi_out"], KD * (b - 1) + 1)
                    pe.wait_ge(S["ot_lo_out"], KD * (b - 1) + 1)
                for m in range(KD):
                    o = bank[4][:, m * (P + 1):(m + 1) * (P + 1)]
                    for t in range(TB):
                        last = mm(o, k_sb[:, t, m * P:(m + 1) * P], v_sb[:, t, m, :],
                                  start=(t == 0), stop=(t == TB - 1))
                last.then_inc(S["kvp_mm"], 1)

            def attend(b):
                pe.wait_ge(S["kvm_out"], b + 1)
                pe.wait_ge(S["q_out"], KD * (b + 1))
                for t in range(TB):
                    if t >= 2:
                        pe.wait_ge(S["o_out"], TB * b + t - 1)
                    elif b >= 1:
                        pe.wait_ge(S["r_out"], TB * b)
                    o = bank[5 + t % 2]
                    for m in range(KD):
                        last = mm(o[:, m * (P + HB):(m + 1) * (P + HB)], q_t[:, m, t * P:(t + 1) * P], kvm[:, m, :],
                                  start=True, stop=True)
                    last.then_inc(S["num_mm"], 1)

            def o_transposed(b):
                if b >= 1:
                    pe.wait_ge(S["lg_out"], b)
                    pe.wait_ge(S["ot_lo_out"], KD * b)
                for t in range(TB):
                    pe.wait_ge(S["o_out"], TB * b + t + 1)
                    for m in range(KD):
                        last = nc.tensor.transpose(bank[(4, 7)[m]][:, t * P:(t + 1) * P],
                                                   o_sb[:, t, m * P:(m + 1) * P], ident)
                last.then_inc(S["ot_mm"], 1)

            def proj_o(b):
                pe.wait_ge(S["ot_hi_out"], KD * (b + 1))
                pe.wait_ge(S["ot_lo_out"], KD * (b + 1))
                if b == 0:
                    pe.wait_ge(S["ow_split"], 2)
                for t in range(TB):
                    if t >= 2:
                        pe.wait_ge(S["r_out"], TB * b + t - 1)
                    o = bank[5 + t % 2][:, 0:D]
                    mm(o, one_f[:, :], b_row[:, 2 * D:3 * D], start=True, stop=False)
                    for k in range(KD):
                        c = slice(t * P, (t + 1) * P)
                        w = slice(WO + k * D, WO + (k + 1) * D)
                        last = split3(o, ot_hi[:, k, c], ot_lo[:, k, c], wa_hi[:, w], wa_lo[:, w], False, k == KD - 1)
                    last.then_inc(S["y_mm"], 1)

            def x1_transposed(b):
                pe.wait_ge(S["x1_out"], TB * (b + 1))
                if b < NB - 1:
                    pe.wait_ge(S["q_out"], KD * (b + 2))
                for t in range(TB):
                    for m in range(KD):
                        last = nc.tensor.transpose(bank[2 + m][:, t * P:(t + 1) * P],
                                                   x1[:, b * TB + t, m * P:(m + 1) * P], ident)
                last.then_inc(S["x1t_mm"], 1)

            def router(b):
                pe.wait_ge(S["x1f_out"], KD * (b + 1))
                for t in range(TB):
                    for k in range(KD):
                        last = mm(bank[4][:, t * NE:(t + 1) * NE], x1_t[:, k, t * P:(t + 1) * P], wg_sb[:, k, :],
                                  start=(k == 0), stop=(k == KD - 1))
                last.then_inc(S["lg_mm"], 1)

            def ranks():
                pe.wait_ge(S["hot_out"], 1)
                o = bank[4][:, 0:T * NE]
                mm(o, tri[:, :], hot_m[:, :], start=True, stop=False, skip_group_check=True)
                for s in range(1, T):
                    mm(o[:, s * NE:], ones[:, :], hot_m[:, 0:(T - s) * NE], start=False, stop=(s == T - 1),
                       skip_group_check=True)
                for t in range(T):
                    last = mm(bank[7][:, 0:NE], ones[:, :], hot_m[:, t * NE:(t + 1) * NE],
                              start=(t == 0), stop=(t == T - 1))
                last.then_inc(S["rank_mm"], 1)

            def shared_gu(b, c):
                i = b * CS + c
                if c == 0:
                    pe.wait_ge(S["x1hi_out"], KD * (b + 1))
                    pe.wait_ge(S["x1lo_out"], KD * (b + 1))
                if i >= 2:
                    pe.wait_ge(S["sh_out"], i - 1)
                for g in range(2):
                    o = bank[2 * (i % 2) + g][:, :]
                    for k in range(KD):
                        w = slice(SH_GU + k * 2 * IS + g * IS + c * P, SH_GU + k * 2 * IS + g * IS + (c + 1) * P)
                        last = split3(o, wf_hi[:, w], wf_lo[:, w], x1t_hi[:, b, k, :], x1t_lo[:, b, k, :],
                                      k == 0, k == KD - 1)
                last.then_inc(S["sgu_mm"], 1)

            def shared_dn(b):
                pe.wait_ge(S["shh_out"], CS * (b + 1))
                pe.wait_ge(S["shl_out"], CS * (b + 1))
                for t in range(TB):
                    if b >= 1:
                        pe.wait_ge(S["sres_out"], TB * (b - 1) + 2 * (t // 2) + 2)
                    o = bank[5 + t // 2][:, (t % 2) * D:(t % 2 + 1) * D]
                    for c in range(CS):
                        w = slice(SH_DN + c * D, SH_DN + (c + 1) * D)
                        n = slice(t * P, (t + 1) * P)
                        last = split3(o, hh_hi[:, c, n], hh_lo[:, c, n], wf_hi[:, w], wf_lo[:, w], c == 0, c == CS - 1)
                    if t % 2:
                        last.then_inc(S["sdn_mm"], 1)

            pe.wait_ge(S["ones_ready"], 2)
            pe.wait_ge(S["bias_ready"], 2)
            pe.wait_ge(S["kvw_split"], 2)
            for t in range(TB):
                proj_kv(0, t)
            proj_q(0)
            pe.wait_ge(S["cst_in"], 16)
            pe.wait_ge(S["small_in"], 32)
            for b in range(NB):
                k_t_v(b)
                if b >= 1:
                    x1_transposed(b - 1)
                if b + 1 < NB:
                    proj_kv(b + 1, 0)
                    proj_kv(b + 1, 1)
                attend(b)
                if b >= 1:
                    router(b - 1)
                if b + 1 < NB:
                    proj_kv(b + 1, 2)
                    proj_kv(b + 1, 3)
                o_transposed(b)
                if b + 1 < NB:
                    proj_q(b + 1)
                proj_o(b)
            pe.wait_ge(S["wf_split"], 2 * (EX // CHUNK))
            shared_gu(0, 0)
            x1_transposed(NB - 1)
            pe.wait_ge(S["ot_lo_out"], KD * NB)
            router(NB - 1)
            pe.wait_ge(S["x1f_out"], KD * NB)
            shared_gu(0, 1)
            shared_gu(0, 2)
            pe.wait_ge(S["lg_out"], NB)
            pe.wait_ge(S["bf_ready"], 2)
            ranks()
            shared_gu(0, 3)
            pe.wait_ge(S["r_out"], T)
            shared_gu(1, 0)
            shared_dn(0)
            for c in range(1, CS):
                shared_gu(1, c)
            shared_dn(1)

            def e_transposed(j, u, rounds, first=False):
                pe.wait_ge(xg_in[u], 16 * rounds)
                if not first:
                    pe.wait_ge(S["xe_lo_out"], j - 1)
                o = bank[(4, 7)[u % 2]]
                for k in range(KD):
                    last = nc.tensor.transpose(o[:, k * P:(k + 1) * P], xg[:, u, k * P:(k + 1) * P], ident)
                last.then_inc(S["xt_e_mm"], 1)

            def weights_of(q):
                word = pe.value_load(te_i[0:1, bass.ds(q, 1)], min_val=0, max_val=(1 << (E_BITS * WORD_TILES)) - 1)
                return [((word >> (E_BITS * n)) & (NE - 1)) * EX_W + EX for n in range(WORD_TILES)]

            def e_gate_up(j, u, w, first=False):
                pe.wait_ge(S["xe_hi_out"], j + 1)
                pe.wait_ge(S["xe_lo_out"], j + 1)
                if not first:
                    pe.wait_ge(S["eh_out"], j - 1)
                o = bank[u % 2][:, 0:2 * IM]
                for k in range(KD):
                    at = w + k * 2 * IM
                    last = split3(o, xe_hi[:, u % 2, k, :], xe_lo[:, u % 2, k, :], wf_hi[:, bass.ds(at, 2 * IM)],
                                  wf_lo[:, bass.ds(at, 2 * IM)], k == 0, k == KD - 1)
                last.then_inc(S["egu_mm"], 1)

            def e_h_transposed(j, u, first=False):
                pe.wait_ge(S["eh_out"], j + 1)
                if not first:
                    pe.wait_ge(S["he_lo_out"], j - 1)
                nc.tensor.transpose(bank[2 + u % 2][:, 0:P], eh[:, u % 2, :], ident).then_inc(S["eht_mm"], 1)

            def e_down(j, u, w, first=False):
                pe.wait_ge(S["he_hi_out"], j + 1)
                pe.wait_ge(S["he_lo_out"], j + 1)
                if not first:
                    pe.wait_ge(S["ey_out"], j - 1)
                at = w + KD * 2 * IM
                split3(bank[5 + u % 2][:, 0:D], he_hi[:, u % 2, :], he_lo[:, u % 2, :], wf_hi[:, bass.ds(at, D)],
                       wf_lo[:, bass.ds(at, D)], True, True).then_inc(S["ey_mm"], 1)

            pe.wait_ge(S["te_out"], 1)
            pe.wait_ge(S["wf_split"], 2 * NCH)
            pe.wait_ge(S["sres_out"], 2 * TB)
            pe.wait_ge(S["sh_out"], 2 * CS)
            at0, at1, at2 = weights_of(0)[RING - 1:]
            e_transposed(0, 0, 1, first=True)
            e_transposed(1, 1, 1, first=True)
            e_gate_up(0, 0, at0, first=True)
            e_transposed(2, 2, 1)
            e_gate_up(1, 1, at1, first=True)
            e_h_transposed(0, 0, first=True)
            e_transposed(3, 3, 1)
            e_gate_up(2, 2, at2)
            e_h_transposed(1, 1, first=True)
            e_down(0, 0, at0, first=True)
            for i in range(NT // RING - 1):
                at = weights_of(i + 1)
                for v in range(RING):
                    s = i * RING + (v + 2)
                    e_transposed(s + 2, v, i + 2)
                    e_gate_up(s + 1, (v + 3) % RING, at[v + 2])
                    e_h_transposed(s, (v + 2) % RING)
                    e_down(s - 1, (v + 1) % RING, at[v])
            at = weights_of(WORDS - 1)
            for s in range(NT - 2, NT + 1):
                if s + 1 < NT:
                    e_gate_up(s + 1, (s + 1) % RING, at[s - NT + RING])
                if s < NT:
                    e_h_transposed(s, s % RING)
                e_down(s - 1, (s - 1) % RING, at[s - NT + 2])

            pe.wait_ge(S["ey_out"], NT)
            shared_gu(2, 0)
            for c in range(1, CS):
                shared_gu(2, c)
            shared_gu(3, 0)
            shared_dn(2)
            for c in range(1, CS):
                shared_gu(3, c)
            shared_dn(3)

        @block.scalar
        def _(act):
            copy, activation = nc.scalar.copy, nc.scalar.activation
            chain = [0]

            def link(ins):
                chain[0] += 1
                ins.then_inc(S["act_chain"], 1)
                act.wait_ge(S["act_chain"], chain[0])

            act.wait_ge(S["b_cleared"], 1)
            act.dma_start(b_raw[0:1, :], batt).then_inc(S["bias_in"], 16)
            act.dma_start(b_raw[32:33, :], batt).then_inc(S["bias_in"], 16)
            act.dma_start(cst[:, :], consts).then_inc(S["cst_in"], 16)
            act.dma_start(bq_sb[:, :], bq).then_inc(S["small_in"], 16)
            act.dma_start(wg_sb[:, :, :], wgate).then_inc(S["small_in"], 16)

            def split_x_hi(b):
                act.wait_ge(xt_in[b % 2], 16 * (b // 2 + 1))
                if b >= 2:
                    act.wait_ge(S["q_mm"], KD * (b - 1))
                for k in range(KD):
                    last = copy(xt_hi[:, b % 2, k, :], xt_raw[:, b % 2, k, :])
                last.then_inc(S["xhi_ready"], 1)

            def kv_out(b, t):
                act.wait_ge(S["kv_mm"], b * TB + t + 1)
                if b >= 1 and t == 0:
                    act.wait_ge(S["kvp_mm"], b)
                o = bank[t % 2]
                activation(k_sb[:, t, :], o[:, 0:D], ACT.Relu, scale=cst[:, C_DEC + t:C_DEC + t + 1])
                copy(v_sb[:, t, :, 0:P], o[:, D:2 * D].rearrange("p (k n) -> p k n", k=KD)).then_inc(S["kv_out"], 1)

            def q_out(b):
                for m in range(KD):
                    act.wait_ge(S["q_mm"], KD * b + m + 1)
                    if b >= 1:
                        act.wait_ge(S["num_mm"], TB * b)
                    activation(q_t[:, m, :], bank[2 + m][:, :], ACT.Relu, bias=bq_sb[:, m:m + 1]).then_inc(S["q_out"], 1)

            def ot_hi_out(b):
                act.wait_ge(S["ot_mm"], b + 1)
                if b >= 1:
                    act.wait_ge(S["y_mm"], TB * b)
                for m in range(KD):
                    copy(ot_hi[:, m, :], bank[(4, 7)[m]][:, :]).then_inc(S["ot_hi_out"], 1)

            def x1f_out(b):
                act.wait_ge(S["x1t_mm"], b + 1)
                if b >= 1:
                    act.wait_ge(S["lg_mm"], b)
                    act.wait_ge(S["x1lo_out"], KD * b)
                for m in range(KD):
                    copy(x1_t[:, m, :], bank[2 + m][:, :]).then_inc(S["x1f_out"], 1)
                act.wait_ge(S["x1f_out"], KD * (b + 1))
                if b == NB - 1:
                    act.wait_ge(S["zero_in"], 16 * (NT // RING))
                for m in range(KD):
                    copy(x1t_hi[:, b, m, :], x1_t[:, m, :]).then_inc(S["x1hi_out"], 1)

            split_x_hi(0)
            act.wait_ge(S["cst_in"], 16)
            for t in range(TB):
                kv_out(0, t)
            split_x_hi(1)
            act.wait_ge(S["small_in"], 32)
            q_out(0)
            for b in range(NB):
                if b >= 1:
                    x1f_out(b - 1)
                if b + 1 < NB:
                    for t in range(TB):
                        kv_out(b + 1, t)
                ot_hi_out(b)
                if b + 1 < NB:
                    q_out(b + 1)
                if b + 2 < NB:
                    split_x_hi(b + 2)

            def shared_sg(b, c):
                i = b * CS + c
                act.wait_ge(S["sgu_mm"], i + 1)
                if i >= 2:
                    act.wait_ge(S["sh_out"], i - 1)
                activation(sg[:, i % 2, :], bank[2 * (i % 2)][:, :], ACT.Silu).then_inc(S["sg_out"], 1)

            def shared_hh(b, c):
                i = b * CS + c
                act.wait_ge(S["sh_out"], i + 1)
                if c == 0 and b >= 1:
                    act.wait_ge(S["sdn_mm"], 2 * b)
                copy(hh_hi[:, c, :], hf[:, i % 2, :]).then_inc(S["shh_out"], 1)

            act.wait_ge(S["q_mm"], KD * NB)
            act.wait_ge(S["xlo_ready"], NB)
            shared_sg(0, 0)
            x1f_out(NB - 1)
            shared_hh(0, 0)
            for c in range(1, 3):
                shared_sg(0, c)
                shared_hh(0, c)
            act.wait_ge(S["tail_norm"], 1)
            activation(wtmp[:, 1, :], wtmp[:, 0, :], ACT.Exp).then_inc(S["exp_out"], 1)
            shared_sg(0, 3)
            shared_hh(0, 3)
            for c in range(CS):
                shared_sg(1, c)
                shared_hh(1, c)

            def e_x_hi(j, u, first=False):
                act.wait_ge(S["xt_e_mm"], j + 1)
                if not first:
                    act.wait_ge(S["egu_mm"], j - 1)
                copy(xe_hi[:, u % 2, :, :], bank[(4, 7)[u % 2]][:, 0:KD * P].rearrange("p (k n) -> p k n", k=KD)
                     ).then_inc(S["xe_hi_out"], 1)

            def e_silu(j, u, first=False):
                act.wait_ge(S["egu_mm"], j + 1)
                if not first:
                    act.wait_ge(S["eh_out"], j - 1)
                activation(eg[:, u % 2, :], bank[u % 2][:, 0:IM], ACT.Silu).then_inc(S["eg_out"], 1)

            def e_h_hi(j, u, first=False):
                act.wait_ge(S["eht_mm"], j + 1)
                if not first:
                    act.wait_ge(S["ey_mm"], j - 1)
                copy(he_hi[:, u % 2, :], bank[2 + u % 2][:, 0:P]).then_inc(S["he_hi_out"], 1)

            def e_y(j, u, rounds):
                act.wait_ge(S["ey_mm"], j + 1)
                if rounds is not None:
                    act.wait_ge(ey_st[u], 16 * rounds)
                copy(ey[:, u, :], bank[5 + u % 2][:, 0:D]).then_inc(S["ey_out"], 1)

            act.wait_ge(S["y_mm"], T)
            act.wait_ge(S["lg_mm"], NB)
            act.wait_ge(S["x1lo_out"], KD * NB)
            act.wait_ge(S["num_mm"], T)
            e_x_hi(0, 0, first=True)
            e_x_hi(1, 1, first=True)
            e_silu(0, 0, first=True)
            e_x_hi(2, 2)
            e_silu(1, 1, first=True)
            e_h_hi(0, 0, first=True)
            e_x_hi(3, 3)
            e_silu(2, 2)
            e_h_hi(1, 1, first=True)
            e_y(0, 0, None)
            for s in range(2, 2 + RING - 1):
                e_x_hi(s + 2, (s + 2) % RING)
                e_silu(s + 1, (s + 1) % RING)
                e_h_hi(s, s % RING)
                e_y(s - 1, s - 1, None)
            with act.Fori(0, NT // RING - 2) as i:
                for v in range(RING):
                    s = i * RING + (v + RING + 1)
                    e_x_hi(s + 2, (v + 3) % RING)
                    e_silu(s + 1, (v + 2) % RING)
                    e_h_hi(s, (v + 1) % RING)
                    e_y(s - 1, v, i + 1)
            for s in range(NT - 3, NT + 1):
                if s + 2 < NT:
                    e_x_hi(s + 2, (s + 2) % RING)
                if s + 1 < NT:
                    e_silu(s + 1, (s + 1) % RING)
                if s < NT:
                    e_h_hi(s, s % RING)
                e_y(s - 1, (s - 1) % RING, (s - 1) // RING)

            def apply_norm(b, t):
                act.wait_ge(S["ln_out"], b + 1)
                activation(x1[:, b * TB + t, :], x1[:, b * TB + t, :], ACT.Identity, scale=nw[:, 1, t:t + 1],
                           bias=nw[:, 3, t:t + 1]).then_inc(S["fin_out"], 1)

            for b in (2, 3):
                for c in range(CS):
                    shared_sg(b, c)
                    shared_hh(b, c)
                    if (b, c) == (2, CS - 1):
                        for t in range(TB):
                            apply_norm(0, t)
                    if (b, c) == (3, 1):
                        for t in range(TB):
                            apply_norm(1, t)
                    if (b, c) == (3, CS - 1):
                        for t in range(TB):
                            apply_norm(2, t)
            for t in range(TB):
                apply_norm(3, t)

        @block.vector
        def _(dve):
            v = nc.vector
            chain = [0]

            def link(ins):
                chain[0] += 1
                ins.then_inc(S["dve_chain"], 1)
                dve.wait_ge(S["dve_chain"], chain[0])

            def split_w(sem_in, at, n, hi_only=False):
                raw = wa_raw[:, at:at + n]
                link(v.tensor_copy(wa_hi[:, at:at + n], raw))
                return v.tensor_tensor(wa_lo[:, at:at + n], raw, wa_hi[:, at:at + n].bitcast(F32), ALU.subtract)

            v.memset(b_raw[:, :], 0.0).then_inc(S["b_cleared"], 1)
            v.memset(v_sb[:, :, :, P:P + 1], 1.0)
            link(v.memset(one_f[:, :].bitcast(F32), 0.0))
            link(v.memset(one_f[0:1, :].bitcast(F32), 1.0))
            v.memset(one_f[32:33, :].bitcast(F32), 1.0).then_inc(S["ones_ready"], 1)
            v.memset(ones[:, :], 1.0).then_inc(S["ones_ready"], 1)
            dve.wait_ge(S["watt_in0"], 16)
            for k in range(KD):
                split_w(None, WKV + k * 2 * D, 2 * D).then_inc(S["kvw_split"], 1)
            dve.wait_ge(S["bias_in"], 32)
            link(v.tensor_copy(b_row[:, :], b_raw[:, :]))
            S_ = v.tensor_tensor(b_row[32:33, :], b_raw[32:33, :], b_row[32:33, :].bitcast(F32), ALU.subtract)
            S_.then_inc(S["bias_ready"], 2)
            dve.wait_ge(S["watt_in1"], 16)
            for k in range(KD):
                split_w(None, WQ + k * D, D).then_inc(S["qw_split"], 1)
            dve.wait_ge(S["watt_in2"], 16)
            for k in range(KD):
                split_w(None, WO + k * D, D).then_inc(S["ow_split"], 1)
            dve.wait_ge(S["cst_in"], 16)
            v.tensor_copy(tri[:, :], cst[:, C_TRI:C_TRI + P]).then_inc(S["bf_ready"], 2)

            def kvm_out(b):
                dve.wait_ge(S["kvp_mm"], b + 1)
                if b >= 1:
                    dve.wait_ge(S["num_mm"], TB * b)
                for m in range(KD):
                    o = bank[4][:, m * (P + 1):(m + 1) * (P + 1)]
                    v.tensor_tensor(kvm[:, m, 0:P], o[:, 0:P], blk, ALU.mult)
                    last = v.tensor_scalar(kvm[:, m, P:P + HB], headm, o[:, P:P + 1], None, ALU.mult)
                last.then_inc(S["kvm_out"], 1)

            def o_out(b, t):
                dve.wait_ge(S["num_mm"], TB * b + t + 1)
                o = bank[5 + t % 2][:, 0:KD * (P + HB)].rearrange("p (k n) -> p k n", k=KD)
                zt = z[:, t % 2]
                link(v.tensor_scalar(zt, o[:, :, P:P + HB], cst[:, C_EPS + t:C_EPS + t + 1], None, ALU.add))
                link(v.reciprocal(zt, zt))
                if t == 0 and b >= 1:
                    dve.wait_ge(S["ot_mm"], b)
                for m in range(KD):
                    last = v.tensor_tensor(
                        o_sb[:, t, m * P:(m + 1) * P].rearrange("p (h e) -> p h e", h=HB),
                        o[:, m, 0:P].rearrange("p (h e) -> p h e", h=HB),
                        zt[:, m, :].unsqueeze(2).broadcast_to([P, HB, DH]), ALU.mult)
                last.then_inc(S["o_out"], 1)

            def ot_lo_out(b):
                if b >= 1:
                    dve.wait_ge(S["y_mm"], TB * b)
                for m in range(KD):
                    dve.wait_ge(S["ot_hi_out"], KD * b + m + 1)
                    v.tensor_tensor(ot_lo[:, m, :], bank[(4, 7)[m]][:, :], ot_hi[:, m, :].bitcast(F32),
                                    ALU.subtract).then_inc(S["ot_lo_out"], 1)

            def rstd(n=TB):
                va, y, t, m = nw[:, 0, :], nw[:, 1, :], nw[:, 2, :], nw[:, 3, :]
                link(v.tensor_scalar(va, mv[:, :, 1], EPS_LN, None, ALU.add))
                link(v.tensor_scalar(nwi[:, :], va.bitcast(I32), 1, None, ALU.logical_shift_right))
                link(v.tensor_scalar(y.bitcast(I32), nwi[:, :], -1.0, float(RSQRT_MAGIC), ALU.mult, ALU.add))
                for _ in range(3):
                    link(v.scalar_tensor_tensor(t, y, -0.5, y, ALU.mult, ALU.mult))
                    link(v.tensor_tensor(t, t, va, ALU.mult))
                    link(v.scalar_tensor_tensor(y, t, 1.5, y, ALU.add, ALU.mult))
                return v.scalar_tensor_tensor(m, mv[:, :, 0], -1.0, y, ALU.mult, ALU.mult)

            def r_out(b, t):
                dve.wait_ge(S["y_mm"], TB * b + t + 1)
                if t == 0:
                    dve.wait_ge(S[f"res_in{b}"], 16)
                r = x1[:, b * TB + t, :]
                v.tensor_tensor(r, bank[5 + t % 2][:, 0:D], r, ALU.add).then_inc(S["r_out"], 1)
                dve.wait_ge(S["r_out"], TB * b + t + 1)
                link(v.bn_stats(stat[:, t, :], r))
                return v.bn_aggr(mv[:, t, :], stat[:, t, :])

            def x1_out(b):
                for t in range(TB):
                    last = r_out(b, t)
                link(last)
                link(rstd())
                for t in range(TB):
                    r = x1[:, b * TB + t, :]
                    v.tensor_scalar(r, r, nw[:, 1, t:t + 1], nw[:, 3, t:t + 1], ALU.mult, ALU.add
                                    ).then_inc(S["x1_out"], 1)

            def top_two(b):
                dve.wait_ge(S["lg_mm"], b + 1)
                ts = slice(b * TB, (b + 1) * TB)
                v.tensor_copy(logit[:, ts, :], bank[4][:, 0:TB * NE].rearrange("p (t e) -> p t e", t=TB)
                              ).then_inc(S["lg_out"], 1)
                dve.wait_ge(S["lg_out"], b + 1)
                for t in range(b * TB, (b + 1) * TB):
                    link(v.max(top_v[:, t, :], logit[:, t, :]))
                    last = v.max_index(top_i[:, t, :], top_v[:, t, :], logit[:, t, :])
                link(last)

            for b in range(NB):
                kvm_out(b)
                for t in range(TB):
                    o_out(b, t)
                if b >= 1:
                    top_two(b - 1)
                ot_lo_out(b)
                x1_out(b)

            def shared_h(b, c):
                i = b * CS + c
                dve.wait_ge(S["sg_out"], i + 1)
                if i >= 2:
                    dve.wait_ge(S["shh_out"], i - 1)
                v.tensor_tensor(hf[:, i % 2, :], bank[2 * (i % 2) + 1][:, :], sg[:, i % 2, :], ALU.mult
                                ).then_inc(S["sh_out"], 1)

            def shared_lo(b, c):
                i = b * CS + c
                dve.wait_ge(S["shh_out"], i + 1)
                v.tensor_tensor(hh_lo[:, c, :], hf[:, i % 2, :], hh_hi[:, c, :].bitcast(F32), ALU.subtract
                                ).then_inc(S["shl_out"], 1)

            def shared_out(b):
                for t in range(TB):
                    if t % 2 == 0:
                        dve.wait_ge(S["sdn_mm"], 2 * b + t // 2 + 1)
                    r = x1[:, b * TB + t, :]
                    if b < 2 and t == 0:
                        dve.wait_ge(S[f"scattered{b}"], 16 * TOPK * TB)
                    v.tensor_tensor(r, bank[5 + t // 2][:, (t % 2) * D:(t % 2 + 1) * D], r, ALU.add
                                    ).then_inc(S["sres_out"], 1)

            def route():
                link(v.tensor_copy(ix_f[:, :, :], top_i[:, :, 0:TOPK]))
                iota = cst[:, C_IOTA:C_IOTA + NE].unsqueeze(1).broadcast_to([P, T, NE])
                for j in range(TOPK):
                    link(v.tensor_tensor(hot[:, j, :].rearrange("p (t e) -> p t e", t=T), iota,
                                         ix_f[:, :, j:j + 1].broadcast_to([P, T, NE]), ALU.is_equal))
                v.tensor_tensor(hot_m[:, :], hot[:, 0, :], hot[:, 1, :], ALU.add).then_inc(S["hot_out"], 1)
                v.tensor_tensor(wtmp[:, 0, :], top_v[:, :, 1], top_v[:, :, 0], ALU.subtract).then_inc(S["tail_norm"], 1)

            def slots():
                c, ct, ci = cnt, cnt_i, None
                dve.wait_ge(S["rank_mm"], 1)
                link(v.tensor_scalar(ct[:, 0, :], bank[7][:, 0:NE], float(P - 1), None, ALU.add))
                link(v.tensor_scalar(ct[:, 1, :], ct[:, 0, :], P.bit_length() - 1, None, ALU.logical_shift_right))
                link(v.tensor_copy(c[:, 0, :], ct[:, 1, :]))
                link(v.memset(c[:, 1, :], 1.0))
                link(v.tensor_tensor_scan(c[:, 2, :], c[:, 1, :], c[:, 0, :], 0.0, ALU.mult, ALU.add))
                link(v.tensor_tensor(c[:, 3, :], c[:, 2, :], c[:, 0, :], ALU.subtract))
                link(v.tensor_scalar(c[:, 4, :], c[:, 3, :], float(P), None, ALU.mult))
                link(v.tensor_tensor(pos[:, :].rearrange("p (t e) -> p t e", t=T),
                                     bank[4][:, 0:T * NE].rearrange("p (t e) -> p t e", t=T),
                                     c[:, 4, :].unsqueeze(1).broadcast_to([P, T, NE]), ALU.add))
                for j in range(TOPK):
                    link(v.tensor_tensor(hot[:, j, :], hot[:, j, :], pos[:, :], ALU.mult))
                    link(v.tensor_reduce(slot_f[:, j, :], hot[:, j, :].rearrange("p (t e) -> p t e", t=T), AX.X, ALU.add))
                v.tensor_copy(slot[:, :, :], slot_f[:, :, :]).then_inc(S["slots_out"], 1)
                link(v.tensor_tensor(te_c[:, :, :], c[0:1, 2, :].unsqueeze(1).broadcast_to([1, NTW, NE]),
                                     cst[0:1, C_TILE:C_TILE + NTW].unsqueeze(2).broadcast_to([1, NTW, NE]), ALU.is_le))
                link(v.tensor_reduce(te_f[:, :], te_c[:, :, :], AX.X, ALU.add))
                link(v.tensor_scalar(te_f[:, :], te_f[:, :], float(NE - 1), None, ALU.min))
                def column(n):
                    return te_f[:, :].rearrange("p (q w) -> p q w", w=RING)[:, n // RING:n // RING + WORDS, n % RING]
                link(v.tensor_copy(te_w[:, :], column(WORD_TILES - 1)))
                for n in reversed(range(WORD_TILES - 1)):
                    dst = te_w if n else te_i
                    ins = v.scalar_tensor_tensor(dst[:, :], te_w[:, :], float(1 << E_BITS), column(n), ALU.mult, ALU.add)
                    if n:
                        link(ins)
                ins.then_inc(S["te_out"], 1)
                dve.wait_ge(S["exp_out"], 1)
                link(v.tensor_scalar(wtmp[:, 2, :], wtmp[:, 1, :], 1.0, None, ALU.add))
                link(v.reciprocal(w_top[:, 0, :], wtmp[:, 2, :]))
                link(v.tensor_tensor(w_top[:, 1, :], wtmp[:, 1, :], w_top[:, 0, :], ALU.mult))

            dve.wait_ge(S["xhi_ready"], NB)
            dve.wait_ge(S["q_mm"], KD * NB)
            dve.wait_ge(S["xlo_ready"], NB)
            shared_h(0, 0)
            top_two(NB - 1)
            route()
            for c in range(3):
                if c:
                    shared_h(0, c)
                shared_lo(0, c)
            slots()
            shared_h(0, 3)
            shared_lo(0, 3)
            shared_h(1, 0)
            shared_out(0)
            shared_lo(1, 0)
            for c in range(1, CS):
                shared_h(1, c)
                shared_lo(1, c)
            shared_out(1)

            def e_x_lo(j, u, first=False):
                dve.wait_ge(S["xe_hi_out"], j + 1)
                if not first:
                    dve.wait_ge(S["egu_mm"], j - 1)
                v.tensor_tensor(xe_lo[:, u % 2, :, :],
                                bank[(4, 7)[u % 2]][:, 0:KD * P].rearrange("p (k n) -> p k n", k=KD),
                                xe_hi[:, u % 2, :, :].bitcast(F32), ALU.subtract).then_inc(S["xe_lo_out"], 1)

            def e_h(j, u, first=False):
                dve.wait_ge(S["eg_out"], j + 1)
                if not first:
                    dve.wait_ge(S["eht_mm"], j - 1)
                v.tensor_tensor(eh[:, u % 2, :], bank[u % 2][:, IM:2 * IM], eg[:, u % 2, :], ALU.mult
                                ).then_inc(S["eh_out"], 1)

            def e_h_lo(j, u, first=False):
                dve.wait_ge(S["he_hi_out"], j + 1)
                if not first:
                    dve.wait_ge(S["ey_mm"], j - 1)
                v.tensor_tensor(he_lo[:, u % 2, :], bank[2 + u % 2][:, 0:P], he_hi[:, u % 2, :].bitcast(F32),
                                ALU.subtract).then_inc(S["he_lo_out"], 1)

            e_x_lo(0, 0, first=True)
            e_x_lo(1, 1, first=True)
            e_h(0, 0, first=True)
            e_x_lo(2, 2)
            e_h(1, 1, first=True)
            e_h_lo(0, 0, first=True)
            e_x_lo(3, 3)
            e_h(2, 2)
            e_h_lo(1, 1, first=True)
            with dve.Fori(0, NT // RING - 1) as i:
                for w in range(RING):
                    s = i * RING + (w + 2)
                    e_x_lo(s + 2, w)
                    e_h(s + 1, (w + 3) % RING)
                    e_h_lo(s, (w + 2) % RING)
            e_h(NT - 1, (NT - 1) % RING)
            for s in (NT - 2, NT - 1):
                e_h_lo(s, s % RING)

            def combine(b, t):
                dve.wait_ge(gath[t], 32 * (b + 1))
                i = b * TB + t
                dve.wait_ge(S["sres_out"], i + 1)
                r = x1[:, i, :]
                link(v.scalar_tensor_tensor(r, g_1[:, t, :], w_top[:, 0, i:i + 1], r, ALU.mult, ALU.add))
                v.scalar_tensor_tensor(r, g_2[:, t, :], w_top[:, 1, i:i + 1], r, ALU.mult, ALU.add
                                       ).then_inc(S["acc_out"], 1)
                dve.wait_ge(S["acc_out"], i + 1)
                link(v.bn_stats(stat[:, t, :], r))
                if b >= 1 and t == 0:
                    dve.wait_ge(S["fin_out"], TB * b)
                link(v.bn_aggr(mv[:, t, :], stat[:, t, :]))
                if t == TB - 1:
                    rstd().then_inc(S["ln_out"], 1)

            for c in range(CS):
                shared_h(2, c)
                shared_lo(2, c)
                combine(0, c)
            shared_h(3, 0)
            shared_out(2)
            shared_lo(3, 0)
            combine(1, 0)
            combine(1, 1)
            shared_h(3, 1)
            shared_lo(3, 1)
            combine(1, 2)
            combine(1, 3)
            shared_h(3, 2)
            shared_lo(3, 2)
            combine(2, 0)
            combine(2, 1)
            shared_h(3, 3)
            shared_lo(3, 3)
            combine(2, 2)
            combine(2, 3)
            shared_out(3)
            for t in range(TB):
                combine(3, t)

        @block.gpsimd
        def _(pool):
            g = nc.gpsimd
            g.memset(stage_zero, 0.0).then_inc(S["pool_chain"], 1)
            pool.wait_ge(S["pool_chain"], 1)
            for j in range(0, NT, RING):
                pool.dma_start(x_scat[j * P:(j + RING) * P, :].rearrange("(a p) d -> p a d", p=P),
                               stage_zero.rearrange("p (a d) -> p a d", a=RING)).then_inc(S["zero_in"], 16)

            def split_x_lo(b):
                pool.wait_ge(S["xhi_ready"], b + 1)
                for k in range(KD):
                    last = g.tensor_tensor(xt_lo[:, b % 2, k, :], xt_raw[:, b % 2, k, :],
                                           xt_hi[:, b % 2, k, :].bitcast(F32), ALU.subtract)
                last.then_inc(S["xlo_ready"], 1)

            def split_chunk(i):
                pool.wait_ge(stage_in[i % 2], 16 * (i // 2 + 1))
                c = slice(i * CHUNK, (i + 1) * CHUNK)
                g.tensor_copy(wf_hi[:, c], stage[:, i % 2, :]).then_inc(S["wf_split"], 1)
                pool.wait_ge(S["wf_split"], 2 * i + 1)
                g.tensor_tensor(wf_lo[:, c], stage[:, i % 2, :], wf_hi[:, c].bitcast(F32), ALU.subtract
                                ).then_inc(S["wf_split"], 1)

            def x1_lo(b):
                pool.wait_ge(S["x1hi_out"], KD * (b + 1))
                for m in range(KD):
                    g.tensor_tensor(x1t_lo[:, b, m, :], x1_t[:, m, :], x1t_hi[:, b, m, :].bitcast(F32),
                                    ALU.subtract).then_inc(S["x1lo_out"], 1)

            per = -(-NCH // NB)
            split_x_lo(0)
            split_x_lo(1)
            done = 0
            for b in range(NB):
                if b >= 1:
                    x1_lo(b - 1)
                for _ in range(per):
                    if done < NCH:
                        split_chunk(done)
                        done += 1
                if b + 2 < NB:
                    split_x_lo(b + 2)
            x1_lo(NB - 1)

            pool.wait_ge(S["zero_in"], 16 * (NT // RING))
            pool.wait_ge(S["slots_out"], 1)
            pool.wait_ge(S["x1_out"], T)
            for t in range(T):
                for j in range(TOPK):
                    pool.indirect_dma_start(out=x_scat, out_offset=bass.IndirectOffsetOnAxis(ap=slot[:, j, t:t + 1], axis=0),
                                            in_=x1[:, t, :], in_offset=None).then_inc(S[f"scattered{t // TB}"], 16)
            for u in range(RING):
                pool.wait_ge(ey_st[u], 16 * (NT // RING))
            for i in range(T):
                b, t = divmod(i, TB)
                if b >= 1:
                    pool.wait_ge(S["acc_out"], i - TB + 1)
                for j, dst in enumerate((g_1, g_2)):
                    pool.indirect_dma_start(out=dst[:, t, :], out_offset=None, in_=y_scat,
                                            in_offset=bass.IndirectOffsetOnAxis(ap=slot[:, j, i:i + 1], axis=0)
                                            ).then_inc(gath[t], 16)


def constants():
    p = np.arange(P)
    c = np.zeros((P, NC_), np.float32)
    c[:, C_ID:C_ID + P] = np.eye(P)
    c[:, C_BLK:C_BLK + P] = p[:, None] // DH == p[None, :] // DH
    c[:, C_HEAD:C_HEAD + HB] = p[:, None] // DH == np.arange(HB)[None, :]
    decay = np.exp(-(np.arange(TB)[None, :] * P + p[:, None]).astype(np.float32) / np.float32(SEQ))
    c[:, C_DEC:C_DEC + TB] = decay
    c[:, C_EPS:C_EPS + TB] = np.float32(EPS_ATT) / decay
    c[:, C_IOTA:C_IOTA + NE] = np.arange(NE)
    c[:, C_TRI:C_TRI + P] = p[:, None] < p[None, :]
    c[:, C_TILE:C_TILE + NTW] = np.arange(NTW) - (RING - 1)
    return c


def rows(w):
    return w.reshape(-1, P, w.shape[-1]).transpose(1, 0, 2).reshape(P, -1)


def kernel(**inputs):
    import concourse.bacc as bacc
    from concourse.bass_utils import run_bass_kernel_spmd

    a = {n.replace("L0_", ""): np.asarray(v) for n, v in inputs.items()}
    x = a["attn_x"]
    wkv = np.concatenate([a["attn_Wk"].T, a["attn_Wv"].T], axis=1)
    gu, dn = a["ffn_w_gate_up"], a["ffn_w_down"]
    arrays = {
        "xT": np.stack([rows(x[b].T) for b in range(NB)]),
        "x": x,
        "watt": np.concatenate([rows(wkv), rows(a["attn_Wq"].T), rows(a["attn_Wo"].T)], axis=1),
        "batt": np.concatenate([a["attn_bk"], a["attn_bv"], a["attn_bo"]])[None, :],
        "bq": rows(a["attn_bq"][:, None]),
        "wffn": np.concatenate([rows(a["ffn_w_sh_gate_up"]), rows(a["ffn_w_sh_down"])]
                               + [rows(w[e]) for e in range(NE) for w in (gu, dn)], axis=1),
        "wgate": rows(a["ffn_w_gate"]).reshape(P, KD, NE),
        "consts": constants(),
    }
    arrays = {n: np.ascontiguousarray(v) for n, v in arrays.items()}
    nc = bacc.Bacc("TRN2", target_bir_lowering=False, num_devices=1)
    aps = [nc.dram_tensor(f"in_{n}", v.shape, mybir.dt.from_np(v.dtype), kind="ExternalInput").ap()
           for n, v in arrays.items()]
    out = nc.dram_tensor("out_0", [NB, SEQ, D], F32, kind="ExternalOutput").ap()
    build(nc, *aps, out)
    r = run_bass_kernel_spmd(nc, [{f"in_{n}": v for n, v in arrays.items()}], core_ids=[0])
    return r.results[0]["out_0"]
```

```python
from contextlib import ExitStack

import numpy as np

import concourse.bass as bass
from concourse import mybir

F32 = mybir.dt.float32
F32R = mybir.dt.float32r
BF16 = mybir.dt.bfloat16
I32 = mybir.dt.int32
U32 = mybir.dt.uint32
ALU = mybir.AluOpType
ACT = mybir.ActivationFunctionType
AX = mybir.AxisListType

P = 128
NB, SEQ, D = 4, 512, 256
KD = D // P
NH, DH = 16, 16
HB = P // DH
NE, TOPK, IM, IS = 8, 2, 128, 512
CS = IS // P
TB = SEQ // P
T = NB * TB
TOK = NB * SEQ
NT = -(-((TOK * TOPK + NE * (P - 1)) // P) // 4) * 4
NSLOT = NT * P
EPS_ATT, EPS_LN = 1e-6, 1e-5
AW = KD * 2 * D + KD * D + KD * D
WKV, WQ, WO = 0, KD * 2 * D, KD * 2 * D + KD * D
SH_GU = 0
SH_DN = SH_GU + KD * 2 * IS
EX = SH_DN + CS * D
EX_W = KD * 2 * IM + D
FW = EX + NE * EX_W
CHUNK = 512
NCH = FW // CHUNK
TAG = 2
DT = D + TAG
FILLS = 5
TAG_LOADS = 4
UNIT = 2
RING = 4
WORDS = NT // RING + 1
WORD_TILES = RING + 2
NTW = (WORDS + 1) * RING
E_BITS = (NE - 1).bit_length()
C_ID, C_BLK = 0, P
C_HEAD = C_BLK + P
C_DEC = C_HEAD + HB
C_EPS = C_DEC + TB
C_IOTA = C_EPS + TB
C_TRI = C_IOTA + NE
C_TILE = C_TRI + P
C_TOK = C_TILE + NTW
C_FILL = C_TOK + T
NC_ = C_FILL + TAG
RSQRT_MAGIC = 0x5F3759DF


def build(nc, xT, x, watt, batt, bq, wffn, wgate, consts, out):
    x_scat = nc.dram_tensor("x_slots", [NSLOT, DT], F32).ap()
    y_scat = nc.dram_tensor("y_pairs", [2 * TOK, D], F32).ap()
    ctx = ExitStack()
    with ctx:
        def sb(name, shape, dt=F32):
            return ctx.enter_context(nc.sbuf_tensor(name, shape, dt))

        def sem(name):
            return ctx.enter_context(nc.semaphore(name))

        cst = sb("cst", [P, NC_])
        tri = sb("tri", [P, P], BF16)
        ones = sb("ones", [P, P], BF16)
        one_f = sb("one_f", [33, P], F32R)
        b_row = sb("b_row", [33, 3 * D], F32R)
        bq_sb = sb("bq_sb", [P, KD])
        wg_sb = sb("wg_sb", [P, KD, NE])
        wa_hi = sb("wa_hi", [P, AW], F32R)
        wa_lo = sb("wa_lo", [P, AW], F32R)
        wf_hi = sb("wf_hi", [P, FW], F32R)
        wf_lo = sb("wf_lo", [P, FW], F32R)
        stage = sb("stage", [P, 2, CHUNK])
        xt_raw = sb("xt_raw", [P, 2, KD, SEQ])
        xt_hi = sb("xt_hi", [P, 2, KD, SEQ], F32R)
        xt_lo = sb("xt_lo", [P, 2, KD, SEQ], F32R)
        x1 = sb("x1", [P, T, DT])
        wa_raw = x1[:, T // 2:, :].rearrange("p t d -> p (t d)")[:, 0:AW]
        k_sb = sb("k_sb", [P, TB, D])
        v_sb = sb("v_sb", [P, TB, KD, P + 1])
        q_t = sb("q_t", [P, KD, SEQ])
        kvm = sb("kvm", [P, KD, P + HB])
        z = sb("z", [P, 2, KD, HB])
        o_sb = sb("o_sb", [P, TB, D])
        ot_hi = sb("ot_hi", [P, KD, SEQ], F32R)
        ot_lo = sb("ot_lo", [P, KD, SEQ], F32R)
        x1_t = sb("x1_t", [P, KD, SEQ])
        x1t_hi = sb("x1t_hi", [P, NB, KD, SEQ], F32R)
        x1t_lo = sb("x1t_lo", [P, NB, KD, SEQ], F32R)
        stat = sb("stat", [P, TB, 6])
        mv = sb("mv", [P, 2, TB, 2])
        nw = sb("nw", [P, 2, 4, TB])
        logit = sb("logit", [P, T, NE])
        top_v = sb("top_v", [P, T, 8])
        top_i = sb("top_i", [P, T, 8], U32)
        ix_f = sb("ix_f", [P, T, TOPK])
        hot = sb("hot", [P, TOPK, T * NE])
        hot_m = sb("hot_m", [P, T * NE], BF16)
        pos = sb("pos", [P, T * NE])
        slot_f = sb("slot_f", [P, TOPK, T])
        slot = sb("slot", [P, TOPK, T], U32)
        w_top = sb("w_top", [P, TOPK, T])
        wtmp = sb("wtmp", [P, 3, T])
        cnt = sb("cnt", [P, 6, NE])
        cnt_i = sb("cnt_i", [P, 2, NE], I32)
        te_c = k_sb[:, 0:2, :].rearrange("p a d -> p (a d)")[:, 0:NTW * NE].rearrange("p (t e) -> p t e", e=NE)
        te_f = sb("te_f", [P, NTW])
        tag = sb("tag", [P, NT, TAG])
        dst_f = sb("dst_f", [P, NT])
        dst = sb("dst", [P, NT], U32)
        te_w = sb("te_w", [1, WORDS])
        te_i = sb("te_i", [1, WORDS], I32)
        b_raw = k_sb[0:33, 0:3, :].rearrange("p a d -> p (a d)")
        fill = x1_t[:, 0, 0:DT]
        sg, hf = xt_raw[:, 0], xt_raw[:, 1]
        hh_hi = xt_hi[:, :, :, :].rearrange("p a k n -> p (a k) n")
        hh_lo = xt_lo[:, :, :, :].rearrange("p a k n -> p (a k) n")
        xg = o_sb
        ey = x1_t[:, :, :].rearrange("p k (a n) -> p (k a) n", a=2)
        xe_hi, xe_lo = (o[:, 0, :].rearrange("p (a k n) -> p a k n", a=2, k=KD) for o in (ot_hi, ot_lo))
        he_hi, he_lo = (o[:, 1, 0:2 * IM].rearrange("p (a n) -> p a n", a=2) for o in (ot_hi, ot_lo))
        eg = q_t[:, 0, 0:2 * IM].rearrange("p (a n) -> p a n", a=2)
        eh = q_t[:, 1, 0:2 * IM].rearrange("p (a n) -> p a n", a=2)
        pair = [k_sb[:, :, :].rearrange("p t d -> p (t d)"),
                v_sb[:, :, :, :].rearrange("p t k n -> p (t k n)")[:, 0:2 * UNIT * D],
                o_sb[:, :, :].rearrange("p t d -> p (t d)"),
                x1_t[:, :, :].rearrange("p k n -> p (k n)"),
                q_t[:, :, :].rearrange("p k n -> p (k n)"),
                stage[:, :, :].rearrange("p a n -> p (a n)")]
        PAIRS = len(pair)
        pair = [o.rearrange("p (i j d) -> p i j d", i=UNIT, j=TOPK) for o in pair]

        ident = cst[:, C_ID:C_ID + P]
        blk = cst[:, C_BLK:C_BLK + P]
        headm = cst[:, C_HEAD:C_HEAD + HB]

        bank = [ctx.enter_context(nc.psum_tensor(f"bank{i}", [P, 512], F32)) for i in range(8)]

        lg_bank = bank[7][:, 0:TB * NE]

        def x1t_bank(b, m):
            return bank[(4, 6)[m]] if b == NB - 1 else bank[2 + m]

        names = """b_cleared cst_in bias_in small_in watt_in0 watt_in1 watt_in2 res_in0 res_in1 res_in2 res_in3
            xt_in0 xt_in1 stage_in0 stage_in1 zero_in
            bf_ready bias_ready ones_ready kvw_split qw_split ow_split wf_split wf_staged_free
            xhi_ready xlo_ready kv_mm kv_out q_mm q_out kvp_mm kvm_out num_mm o_out ot_mm ot_hi_out ot_lo_out
            y_mm r_out x1_out x1t_mm x1f_out x1hi_out x1lo_out lg_mm lg_out
            hot_out rank_mm slots_out exp_in exp_out te_out scattered0 scattered1 scattered2 scattered3
            sgu_mm sg_out sh_out shh_out shl_out sdn_mm sres_out
            xt_e_mm xe_hi_out xe_lo_out egu_mm eg_out eh_out eht_mm he_hi_out he_lo_out ey_mm ey_out
            fill_made tags_out dst_out bn_out mom_out nw_out acc_out stat_out ln_out ln_last_out fin_out stored
            dve_chain pool_chain act_chain tail_norm""".split()
        S = {n: sem(n) for n in names}
        xg_in = [sem(f"xg_in{u}") for u in range(RING)]
        ey_st = [sem(f"ey_st{u}") for u in range(RING)]
        pair_in = [sem(f"pair_in{n}") for n in range(T // UNIT)]
        tag_in = [sem(f"tag_in{n}") for n in range(TAG_LOADS)]
        xt_in = [S["xt_in0"], S["xt_in1"]]
        stage_in = [S["stage_in0"], S["stage_in1"]]

        def rstd(v, link, h, fused):
            va, y, t, m = (nw[:, h, n, :] for n in range(4))
            link(v.tensor_scalar(va, mv[:, h, :, 1], EPS_LN, None, ALU.add))
            link(v.tensor_scalar(y.bitcast(I32), va.bitcast(I32), -0.5, float(RSQRT_MAGIC), ALU.mult, ALU.add))
            for _ in range(3):
                if fused:
                    link(v.scalar_tensor_tensor(t, y, -0.5, y, ALU.mult, ALU.mult))
                    link(v.tensor_tensor(t, t, va, ALU.mult))
                    link(v.scalar_tensor_tensor(y, t, 1.5, y, ALU.add, ALU.mult))
                else:
                    link(v.tensor_tensor(t, y, y, ALU.mult))
                    link(v.tensor_tensor(t, t, va, ALU.mult))
                    link(v.tensor_scalar(t, t, -0.5, 1.5, ALU.mult, ALU.add))
                    link(v.tensor_tensor(y, t, y, ALU.mult))
            if fused:
                return v.scalar_tensor_tensor(m, mv[:, h, :, 0], -1.0, y, ALU.mult, ALU.mult)
            link(v.tensor_tensor(m, mv[:, h, :, 0], y, ALU.mult))
            return v.tensor_scalar(m, m, -1.0, None, ALU.mult)

        block = ctx.enter_context(nc.Block())

        @block.sync
        def _(sp):
            def load_xt(b):
                sp.dma_start(xt_raw[:, b % 2], xT[b].rearrange("p (k n) -> p k n", k=KD)).then_inc(xt_in[b % 2], 16)

            def load_res(b):
                sp.dma_start(x1[:, b * TB:(b + 1) * TB, 0:D], x[b].rearrange("(t p) d -> p t d", p=P)
                             ).then_inc(S[f"res_in{b}"], 16)

            load_xt(0)
            sp.dma_start(wa_raw[:, WKV:WQ], watt[:, WKV:WQ]).then_inc(S["watt_in0"], 16)
            sp.dma_start(wa_raw[:, WQ:WO], watt[:, WQ:WO]).then_inc(S["watt_in1"], 16)
            load_xt(1)
            sp.dma_start(wa_raw[:, WO:AW], watt[:, WO:AW]).then_inc(S["watt_in2"], 16)
            load_res(0)
            load_res(1)

            def load_chunk(i):
                if i >= 2:
                    sp.wait_ge(S["wf_split"], 2 * (i - 1))
                sp.dma_start(stage[:, i % 2, :], wffn[:, i * CHUNK:(i + 1) * CHUNK]).then_inc(stage_in[i % 2], 16)

            for i in range(NCH):
                if i < FILLS:
                    if i == 0:
                        sp.wait_ge(S["fill_made"], 1)
                    n = NT // FILLS
                    sp.dma_start(x_scat[i * n * P:(i + 1) * n * P, :].rearrange("(a p) d -> p a d", p=P),
                                 fill.unsqueeze(1).broadcast_to([P, n, DT])).then_inc(S["zero_in"], 16)
                if i == 6:
                    sp.wait_ge(S["ow_split"], 2)
                    load_res(2)
                    load_res(3)
                if i in (2, 6):
                    b = 2 if i == 2 else 3
                    sp.wait_ge(S["xhi_ready"], b - 1)
                    sp.wait_ge(S["xlo_ready"], b - 1)
                    load_xt(b)
                load_chunk(i)

            for b in range(NB):
                sp.wait_ge(S[f"scattered{b}"], 16 * TOPK * TB)

            def load_tile(j, u, first=False):
                if not first:
                    sp.wait_ge(S["xt_e_mm"], j - RING + 1)
                sp.dma_start(xg[:, u, :], x_scat[bass.ds(j * P, P), 0:D]).then_inc(xg_in[u], 16)

            for u in range(RING):
                load_tile(u, u, first=True)
            for n in range(TAG_LOADS):
                j = slice(n * NT // TAG_LOADS, (n + 1) * NT // TAG_LOADS)
                sp.dma_start(tag[:, j, :], x_scat.rearrange("(t p) d -> p t d", p=P)[:, j, D:DT]).then_inc(tag_in[n], 16)
            with sp.Fori(0, NT // RING - 1) as i:
                for v in range(RING):
                    load_tile(i * RING + (RING + v), v)

            for u in range(RING):
                sp.wait_ge(ey_st[u], 16 * (NT // RING))
            for n in range(T // UNIT):
                if n >= PAIRS:
                    sp.wait_ge(S["acc_out"], UNIT * (n - PAIRS + 1))
                rows = slice(2 * n * UNIT * P, 2 * (n + 1) * UNIT * P)
                sp.dma_start(pair[n % PAIRS].rearrange("p i j d -> p i (j d)"),
                             y_scat[rows, :].rearrange("(i p j) d -> p i (j d)", p=P, j=TOPK)).then_inc(pair_in[n], 16)
            for b in range(NB):
                sp.wait_ge(S["fin_out"], TB * (b + 1))
                sp.dma_start(out[b].rearrange("(t p) d -> p t d", p=P), x1[:, b * TB:(b + 1) * TB, 0:D]
                             ).then_inc(S["stored"], 16)
            sp.wait_ge(S["stored"], 16 * NB)

        @block.tensor
        def _(pe):
            mm = nc.tensor.matmul

            def split3(o, w_hi, w_lo, m_hi, m_lo, start, stop):
                mm(o, w_hi, m_hi, start=start, stop=False)
                mm(o, w_hi, m_lo, start=False, stop=False)
                return mm(o, w_lo, m_hi, start=False, stop=stop)

            def proj_kv(b, t):
                i = b * TB + t
                if t == 0:
                    pe.wait_ge(S["xhi_ready"], b + 1)
                    pe.wait_ge(S["xlo_ready"], b + 1)
                if i >= 2:
                    pe.wait_ge(S["kv_out"], i - 1)
                o = bank[t % 2][:, :]
                for k in range(KD):
                    if i == 0:
                        pe.wait_ge(S["kvw_split"], k + 1)
                    c = slice(t * P, (t + 1) * P)
                    w = slice(WKV + k * 2 * D, WKV + (k + 1) * 2 * D)
                    split3(o, xt_hi[:, b % 2, k, c], xt_lo[:, b % 2, k, c], wa_hi[:, w], wa_lo[:, w], k == 0, False)
                if i == 0:
                    pe.wait_ge(S["ones_ready"], 2)
                    pe.wait_ge(S["bias_ready"], 1)
                mm(o, one_f[:, :], b_row[:, 0:2 * D], start=False, stop=True).then_inc(S["kv_mm"], 1)

            def proj_q(b):
                if b == 0:
                    pe.wait_ge(S["qw_split"], 2)
                for m in range(KD):
                    if b >= 1:
                        pe.wait_ge(S["q_out"], KD * (b - 1) + m + 1)
                    if b >= 3:
                        pe.wait_ge(S["x1f_out"], KD * (b - 3) + m + 1)
                    o = bank[2 + m][:, :]
                    for k in range(KD):
                        w = slice(WQ + k * D + m * P, WQ + k * D + (m + 1) * P)
                        last = split3(o, wa_hi[:, w], wa_lo[:, w], xt_hi[:, b % 2, k, :], xt_lo[:, b % 2, k, :],
                                      k == 0, k == KD - 1)
                    last.then_inc(S["q_mm"], 1)

            def k_t_v(b):
                pe.wait_ge(S["kv_out"], TB * (b + 1))
                if b >= 1:
                    pe.wait_ge(S["ot_hi_out"], KD * (b - 1) + 1)
                    pe.wait_ge(S["ot_lo_out"], KD * (b - 1) + 1)
                for m in range(KD):
                    o = bank[4][:, m * (P + 1):(m + 1) * (P + 1)]
                    for t in range(TB):
                        last = mm(o, k_sb[:, t, m * P:(m + 1) * P], v_sb[:, t, m, :],
                                  start=(t == 0), stop=(t == TB - 1))
                last.then_inc(S["kvp_mm"], 1)

            def attend(b, ts):
                pe.wait_ge(S["kvm_out"], b + 1)
                pe.wait_ge(S["q_out"], KD * (b + 1))
                for t in ts:
                    if t >= 2:
                        pe.wait_ge(S["o_out"], TB * b + t - 1)
                    elif b >= 1:
                        pe.wait_ge(S["r_out"], TB * b)
                    o = bank[5 + t % 2]
                    for m in range(KD):
                        last = mm(o[:, m * (P + HB):(m + 1) * (P + HB)], q_t[:, m, t * P:(t + 1) * P], kvm[:, m, :],
                                  start=True, stop=True)
                    last.then_inc(S["num_mm"], 1)

            def o_transposed(b):
                if b >= 1:
                    pe.wait_ge(S["ot_lo_out"], KD * b)
                if b >= 2:
                    pe.wait_ge(S["lg_out"], b - 1)
                for t in range(TB):
                    pe.wait_ge(S["o_out"], TB * b + t + 1)
                    for m in range(KD):
                        last = nc.tensor.transpose(bank[(4, 7)[m]][:, t * P:(t + 1) * P],
                                                   o_sb[:, t, m * P:(m + 1) * P], ident)
                last.then_inc(S["ot_mm"], 1)

            def proj_o(b):
                pe.wait_ge(S["ot_hi_out"], KD * (b + 1))
                pe.wait_ge(S["ot_lo_out"], KD * (b + 1))
                if b == 0:
                    pe.wait_ge(S["ow_split"], 2)
                for t in range(TB):
                    if t >= 2:
                        pe.wait_ge(S["r_out"], TB * b + t - 1)
                    o = bank[5 + t % 2][:, 0:D]
                    mm(o, one_f[:, :], b_row[:, 2 * D:3 * D], start=True, stop=False)
                    for k in range(KD):
                        c = slice(t * P, (t + 1) * P)
                        w = slice(WO + k * D, WO + (k + 1) * D)
                        last = split3(o, ot_hi[:, k, c], ot_lo[:, k, c], wa_hi[:, w], wa_lo[:, w], False, k == KD - 1)
                    last.then_inc(S["y_mm"], 1)

            def x1_transposed(b):
                pe.wait_ge(S["x1_out"], TB * (b + 1))
                if b < NB - 2:
                    pe.wait_ge(S["q_out"], KD * (b + 3))
                for t in range(TB):
                    for m in range(KD):
                        last = nc.tensor.transpose(x1t_bank(b, m)[:, t * P:(t + 1) * P],
                                                   x1[:, b * TB + t, m * P:(m + 1) * P], ident)
                last.then_inc(S["x1t_mm"], 1)

            def router(b):
                pe.wait_ge(S["x1f_out"], KD * (b + 1))
                pe.wait_ge(S["ot_lo_out"], KD * min(b + 2, NB))
                if b >= 1:
                    pe.wait_ge(S["lg_out"], b)
                for t in range(TB):
                    for k in range(KD):
                        last = mm(lg_bank[:, t * NE:(t + 1) * NE], x1_t[:, k, t * P:(t + 1) * P], wg_sb[:, k, :],
                                  start=(k == 0), stop=(k == KD - 1))
                last.then_inc(S["lg_mm"], 1)

            def ranks():
                pe.wait_ge(S["hot_out"], 1)
                o = bank[4][:, 0:(T + 1) * NE]
                mm(o[:, 0:T * NE], tri[:, :], hot_m[:, :], start=True, stop=False, skip_group_check=True)
                for s in range(1, T + 1):
                    last = mm(o[:, s * NE:], ones[:, :], hot_m[:, 0:(T + 1 - s) * NE], start=False, stop=(s == T),
                              skip_group_check=True)
                last.then_inc(S["rank_mm"], 1)

            def shared_gu(b, c, part=None):
                i = b * CS + c
                if c == 0:
                    pe.wait_ge(S["x1hi_out"], KD * (b + 1))
                    pe.wait_ge(S["x1lo_out"], KD * (b + 1))
                if i >= 2:
                    pe.wait_ge(S["sh_out"], i - 1)
                for g in range(2) if part is None else (part,):
                    o = bank[2 * (i % 2) + g][:, :]
                    for k in range(KD):
                        w = slice(SH_GU + k * 2 * IS + g * IS + c * P, SH_GU + k * 2 * IS + g * IS + (c + 1) * P)
                        last = split3(o, wf_hi[:, w], wf_lo[:, w], x1t_hi[:, b, k, :], x1t_lo[:, b, k, :],
                                      k == 0, k == KD - 1)
                if part != 0:
                    last.then_inc(S["sgu_mm"], 1)

            def shared_dn(b):
                pe.wait_ge(S["shh_out"], CS * (b + 1))
                pe.wait_ge(S["shl_out"], CS * (b + 1))
                for t in range(TB):
                    if b >= 1:
                        pe.wait_ge(S["sres_out"], TB * (b - 1) + 2 * (t // 2) + 2)
                    o = bank[5 + t // 2][:, (t % 2) * D:(t % 2 + 1) * D]
                    for c in range(CS):
                        w = slice(SH_DN + c * D, SH_DN + (c + 1) * D)
                        n = slice(t * P, (t + 1) * P)
                        last = split3(o, hh_hi[:, c, n], hh_lo[:, c, n], wf_hi[:, w], wf_lo[:, w], c == 0, c == CS - 1)
                    if t % 2:
                        last.then_inc(S["sdn_mm"], 1)

            for t in range(TB):
                proj_kv(0, t)
            proj_q(0)
            pe.wait_ge(S["cst_in"], 16)
            pe.wait_ge(S["small_in"], 32)
            for b in range(NB):
                more = b + 1 < NB
                k_t_v(b)
                if more:
                    proj_kv(b + 1, 0)
                    proj_kv(b + 1, 1)
                else:
                    pe.wait_ge(S["kv_out"], T)
                    pe.wait_ge(S["wf_split"], 2 * (EX // CHUNK))
                    shared_gu(0, 0)
                attend(b, range(0, 2))
                if more:
                    proj_kv(b + 1, 2)
                    proj_kv(b + 1, 3)
                else:
                    x1_transposed(b - 1)
                attend(b, range(2, TB))
                if more:
                    proj_q(b + 1)
                o_transposed(b)
                if more and b >= 1:
                    x1_transposed(b - 1)
                if not more:
                    pe.wait_ge(S["x1f_out"], KD * (NB - 1))
                    shared_gu(0, 1)
                proj_o(b)
                if b >= 1:
                    router(b - 1)
            shared_gu(0, 2)
            x1_transposed(NB - 1)
            shared_gu(0, 3, part=0)
            router(NB - 1)
            shared_gu(0, 3, part=1)
            shared_gu(1, 0, part=0)
            pe.wait_ge(S["lg_out"], NB)
            pe.wait_ge(S["bf_ready"], 1)
            ranks()
            shared_gu(1, 0, part=1)
            shared_gu(1, 1)
            pe.wait_ge(S["r_out"], T)
            shared_dn(0)
            for b in (1, 2):
                shared_gu(b, 2)
                shared_gu(b, 3)
                if b < 2:
                    shared_gu(b + 1, 0)
                    shared_gu(b + 1, 1)
                shared_dn(b)

            def e_transposed(j, u, rounds, first=False):
                pe.wait_ge(xg_in[u], 16 * rounds)
                if not first:
                    pe.wait_ge(S["xe_lo_out"], j - 1)
                o = bank[(4, 7)[u % 2]]
                for k in range(KD):
                    last = nc.tensor.transpose(o[:, k * P:(k + 1) * P], xg[:, u, k * P:(k + 1) * P], ident)
                last.then_inc(S["xt_e_mm"], 1)

            def weights_of(q):
                word = pe.value_load(te_i[0:1, bass.ds(q, 1)], min_val=0, max_val=(1 << (E_BITS * WORD_TILES)) - 1)
                return [((word >> (E_BITS * n)) & (NE - 1)) * EX_W + EX for n in range(WORD_TILES)]

            def e_gate_up(j, u, w, first=False):
                pe.wait_ge(S["xe_hi_out"], j + 1)
                pe.wait_ge(S["xe_lo_out"], j + 1)
                if not first:
                    pe.wait_ge(S["eh_out"], j - 1)
                o = bank[u % 2][:, 0:2 * IM]
                for k in range(KD):
                    at = w + k * 2 * IM
                    last = split3(o, xe_hi[:, u % 2, k, :], xe_lo[:, u % 2, k, :], wf_hi[:, bass.ds(at, 2 * IM)],
                                  wf_lo[:, bass.ds(at, 2 * IM)], k == 0, k == KD - 1)
                last.then_inc(S["egu_mm"], 1)

            def e_h_transposed(j, u, first=False):
                pe.wait_ge(S["eh_out"], j + 1)
                if not first:
                    pe.wait_ge(S["he_lo_out"], j - 1)
                nc.tensor.transpose(bank[2 + u % 2][:, 0:P], eh[:, u % 2, :], ident).then_inc(S["eht_mm"], 1)

            def e_down(j, u, w, first=False):
                pe.wait_ge(S["he_hi_out"], j + 1)
                pe.wait_ge(S["he_lo_out"], j + 1)
                if not first:
                    pe.wait_ge(S["ey_out"], j - 1)
                at = w + KD * 2 * IM
                split3(bank[5 + u % 2][:, 0:D], he_hi[:, u % 2, :], he_lo[:, u % 2, :], wf_hi[:, bass.ds(at, D)],
                       wf_lo[:, bass.ds(at, D)], True, True).then_inc(S["ey_mm"], 1)

            pe.wait_ge(S["te_out"], 1)
            pe.wait_ge(S["wf_split"], 2 * NCH)
            pe.wait_ge(S["sres_out"], 3 * TB)
            pe.wait_ge(S["sh_out"], 3 * CS)
            at0, at1, at2 = weights_of(0)[RING - 1:]
            e_transposed(0, 0, 1, first=True)
            e_transposed(1, 1, 1, first=True)
            e_gate_up(0, 0, at0, first=True)
            e_transposed(2, 2, 1)
            e_gate_up(1, 1, at1, first=True)
            e_h_transposed(0, 0, first=True)
            e_transposed(3, 3, 1)
            e_gate_up(2, 2, at2)
            e_h_transposed(1, 1, first=True)
            e_down(0, 0, at0, first=True)
            for i in range(NT // RING - 1):
                at = weights_of(i + 1)
                for v in range(RING):
                    s = i * RING + (v + 2)
                    e_transposed(s + 2, v, i + 2)
                    e_gate_up(s + 1, (v + 3) % RING, at[v + 2])
                    e_h_transposed(s, (v + 2) % RING)
                    e_down(s - 1, (v + 1) % RING, at[v])
            at = weights_of(WORDS - 1)
            for s in range(NT - 2, NT + 1):
                if s + 1 < NT:
                    e_gate_up(s + 1, (s + 1) % RING, at[s - NT + RING])
                if s < NT:
                    e_h_transposed(s, s % RING)
                e_down(s - 1, (s - 1) % RING, at[s - NT + 2])

            pe.wait_ge(S["ey_out"], NT)
            for c in range(CS):
                shared_gu(3, c)
            shared_dn(3)

        @block.scalar
        def _(act):
            copy, activation = nc.scalar.copy, nc.scalar.activation
            chain = [0]

            def link(ins):
                chain[0] += 1
                ins.then_inc(S["act_chain"], 1)
                act.wait_ge(S["act_chain"], chain[0])

            act.wait_ge(S["b_cleared"], 1)
            act.dma_start(b_raw[0:1, :], batt).then_inc(S["bias_in"], 16)
            act.dma_start(b_raw[32:33, :], batt).then_inc(S["bias_in"], 16)
            act.dma_start(cst[:, :], consts).then_inc(S["cst_in"], 16)
            act.dma_start(bq_sb[:, :], bq).then_inc(S["small_in"], 16)
            act.dma_start(wg_sb[:, :, :], wgate).then_inc(S["small_in"], 16)

            def split_x_hi(b):
                act.wait_ge(xt_in[b % 2], 16 * (b // 2 + 1))
                if b >= 2:
                    act.wait_ge(S["q_mm"], KD * (b - 1))
                for k in range(KD):
                    last = copy(xt_hi[:, b % 2, k, :], xt_raw[:, b % 2, k, :])
                last.then_inc(S["xhi_ready"], 1)

            def kv_out(b, t):
                act.wait_ge(S["kv_mm"], b * TB + t + 1)
                if b >= 1 and t == 0:
                    act.wait_ge(S["kvp_mm"], b)
                o = bank[t % 2]
                activation(k_sb[:, t, :], o[:, 0:D], ACT.Relu, scale=cst[:, C_DEC + t:C_DEC + t + 1])
                copy(v_sb[:, t, :, 0:P], o[:, D:2 * D].rearrange("p (k n) -> p k n", k=KD)).then_inc(S["kv_out"], 1)

            def q_out(b):
                for m in range(KD):
                    act.wait_ge(S["q_mm"], KD * b + m + 1)
                    if b >= 1:
                        act.wait_ge(S["num_mm"], TB * b)
                    activation(q_t[:, m, :], bank[2 + m][:, :], ACT.Relu, bias=bq_sb[:, m:m + 1]).then_inc(S["q_out"], 1)

            def ot_hi_out(b):
                act.wait_ge(S["ot_mm"], b + 1)
                if b >= 1:
                    act.wait_ge(S["y_mm"], TB * b)
                for m in range(KD):
                    copy(ot_hi[:, m, :], bank[(4, 7)[m]][:, :]).then_inc(S["ot_hi_out"], 1)

            def x1_apply(b):
                act.wait_ge(S["nw_out"], b + 1)
                for t in range(TB):
                    r = x1[:, b * TB + t, 0:D]
                    activation(r, r, ACT.Identity, scale=nw[:, 0, 1, t:t + 1], bias=nw[:, 0, 3, t:t + 1]
                               ).then_inc(S["x1_out"], 1)

            def x1f_out(b):
                act.wait_ge(S["x1t_mm"], b + 1)
                if b == 0:
                    act.wait_ge(S["zero_in"], 16 * FILLS)
                if b >= 1:
                    act.wait_ge(S["lg_mm"], b)
                    act.wait_ge(S["x1lo_out"], KD * b)
                for m in range(KD):
                    copy(x1_t[:, m, :], x1t_bank(b, m)[:, :]).then_inc(S["x1f_out"], 1)
                act.wait_ge(S["x1f_out"], KD * (b + 1))
                for m in range(KD):
                    copy(x1t_hi[:, b, m, :], x1_t[:, m, :]).then_inc(S["x1hi_out"], 1)

            def shared_sg(b, c):
                i = b * CS + c
                act.wait_ge(S["sgu_mm"], i + 1)
                if i >= 2:
                    act.wait_ge(S["sh_out"], i - 1)
                activation(sg[:, i % 2, :], bank[2 * (i % 2)][:, :], ACT.Silu).then_inc(S["sg_out"], 1)

            def shared_hh(b, c):
                i = b * CS + c
                act.wait_ge(S["sh_out"], i + 1)
                if c == 0 and b >= 1:
                    act.wait_ge(S["sdn_mm"], 2 * b)
                copy(hh_hi[:, c, :], hf[:, i % 2, :]).then_inc(S["shh_out"], 1)

            split_x_hi(0)
            act.wait_ge(S["cst_in"], 16)
            for t in range(TB):
                kv_out(0, t)
            split_x_hi(1)
            act.wait_ge(S["small_in"], 32)
            q_out(0)
            for b in range(NB - 1):
                for t in range(TB):
                    kv_out(b + 1, t)
                if b >= 1:
                    x1_apply(b - 1)
                if b + 2 < NB:
                    split_x_hi(b + 2)
                q_out(b + 1)
                ot_hi_out(b)
                if b >= 1:
                    x1f_out(b - 1)
            act.wait_ge(S["q_mm"], KD * NB)
            act.wait_ge(S["xlo_ready"], NB)
            shared_sg(0, 0)
            x1_apply(NB - 2)
            x1f_out(NB - 2)
            ot_hi_out(NB - 1)
            shared_sg(0, 1)
            shared_hh(0, 0)
            shared_hh(0, 1)
            shared_sg(0, 2)
            x1_apply(NB - 1)
            x1f_out(NB - 1)
            shared_hh(0, 2)
            shared_sg(0, 3)
            shared_hh(0, 3)
            shared_sg(1, 0)
            shared_sg(1, 1)
            act.wait_ge(S["tail_norm"], 1)
            activation(wtmp[:, 1, :], wtmp[:, 0, :], ACT.Exp).then_inc(S["exp_out"], 1)
            for b in (1, 2):
                shared_hh(b, 0)
                shared_hh(b, 1)
                for c in (2, 3):
                    shared_sg(b, c)
                    shared_hh(b, c)
                if b < 2:
                    shared_sg(b + 1, 0)
                    shared_sg(b + 1, 1)

            def e_x_hi(j, u, first=False):
                act.wait_ge(S["xt_e_mm"], j + 1)
                if not first:
                    act.wait_ge(S["egu_mm"], j - 1)
                copy(xe_hi[:, u % 2, :, :], bank[(4, 7)[u % 2]][:, 0:KD * P].rearrange("p (k n) -> p k n", k=KD)
                     ).then_inc(S["xe_hi_out"], 1)

            def e_silu(j, u, first=False):
                act.wait_ge(S["egu_mm"], j + 1)
                if not first:
                    act.wait_ge(S["eh_out"], j - 1)
                activation(eg[:, u % 2, :], bank[u % 2][:, 0:IM], ACT.Silu).then_inc(S["eg_out"], 1)

            def e_h_hi(j, u, first=False):
                act.wait_ge(S["eht_mm"], j + 1)
                if not first:
                    act.wait_ge(S["ey_mm"], j - 1)
                copy(he_hi[:, u % 2, :], bank[2 + u % 2][:, 0:P]).then_inc(S["he_hi_out"], 1)

            def e_y(j, u, rounds):
                act.wait_ge(S["ey_mm"], j + 1)
                if rounds is not None:
                    act.wait_ge(ey_st[u], 16 * rounds)
                copy(ey[:, u, :], bank[5 + u % 2][:, 0:D]).then_inc(S["ey_out"], 1)

            act.wait_ge(S["y_mm"], T)
            act.wait_ge(S["lg_mm"], NB)
            act.wait_ge(S["x1lo_out"], KD * NB)
            act.wait_ge(S["num_mm"], T)
            e_x_hi(0, 0, first=True)
            e_x_hi(1, 1, first=True)
            e_silu(0, 0, first=True)
            e_x_hi(2, 2)
            e_silu(1, 1, first=True)
            e_h_hi(0, 0, first=True)
            e_x_hi(3, 3)
            e_silu(2, 2)
            e_h_hi(1, 1, first=True)
            e_y(0, 0, None)
            for s in range(2, 2 + RING - 1):
                e_x_hi(s + 2, (s + 2) % RING)
                e_silu(s + 1, (s + 1) % RING)
                e_h_hi(s, s % RING)
                e_y(s - 1, s - 1, None)
            with act.Fori(0, NT // RING - 2) as i:
                for v in range(RING):
                    s = i * RING + (v + RING + 1)
                    e_x_hi(s + 2, (v + 3) % RING)
                    e_silu(s + 1, (v + 2) % RING)
                    e_h_hi(s, (v + 1) % RING)
                    e_y(s - 1, v, i + 1)
            for s in range(NT - 3, NT + 1):
                if s + 2 < NT:
                    e_x_hi(s + 2, (s + 2) % RING)
                if s + 1 < NT:
                    e_silu(s + 1, (s + 1) % RING)
                if s < NT:
                    e_h_hi(s, s % RING)
                e_y(s - 1, (s - 1) % RING, (s - 1) // RING)

            def apply_norm(b, t):
                if b < NB - 1:
                    act.wait_ge(S["ln_out"], b + 1)
                else:
                    act.wait_ge(S["ln_last_out"], 1)
                r = x1[:, b * TB + t, 0:D]
                activation(r, r, ACT.Identity, scale=nw[:, b % 2, 1, t:t + 1], bias=nw[:, b % 2, 3, t:t + 1]
                           ).then_inc(S["fin_out"], 1)

            for c in range(CS):
                shared_sg(3, c)
                shared_hh(3, c)
            for b in range(NB):
                for t in range(TB):
                    apply_norm(b, t)

        @block.vector
        def _(dve):
            v = nc.vector
            chain = [0]

            def link(*instructions):
                for ins in instructions:
                    chain[0] += 1
                    ins.then_inc(S["dve_chain"], 1)
                dve.wait_ge(S["dve_chain"], chain[0])

            def split_w(at, n):
                raw = wa_raw[:, at:at + n]
                link(v.tensor_copy(wa_hi[:, at:at + n], raw))
                return v.tensor_tensor(wa_lo[:, at:at + n], raw, wa_hi[:, at:at + n].bitcast(F32), ALU.subtract)

            v.memset(b_raw[:, :], 0.0).then_inc(S["b_cleared"], 1)
            v.memset(v_sb[:, :, :, P:P + 1], 1.0)
            link(v.memset(one_f[:, :].bitcast(F32), 0.0))
            link(v.memset(one_f[0:1, :].bitcast(F32), 1.0))
            v.memset(one_f[32:33, :].bitcast(F32), 1.0).then_inc(S["ones_ready"], 1)
            v.memset(ones[:, :], 1.0).then_inc(S["ones_ready"], 1)
            dve.wait_ge(S["watt_in0"], 16)
            for k in range(KD):
                split_w(WKV + k * 2 * D, 2 * D).then_inc(S["kvw_split"], 1)
            dve.wait_ge(S["xhi_ready"], 1)
            for k in range(KD):
                ins = v.tensor_tensor(xt_lo[:, 0, k, :], xt_raw[:, 0, k, :], xt_hi[:, 0, k, :].bitcast(F32), ALU.subtract)
            ins.then_inc(S["xlo_ready"], 1)
            dve.wait_ge(S["bias_in"], 32)
            link(v.tensor_copy(b_row[:, :], b_raw[:, :]))
            v.tensor_tensor(b_row[32:33, :], b_raw[32:33, :], b_row[32:33, :].bitcast(F32), ALU.subtract
                            ).then_inc(S["bias_ready"], 1)
            dve.wait_ge(S["watt_in1"], 16)
            for k in range(KD):
                split_w(WQ + k * D, D).then_inc(S["qw_split"], 1)
            dve.wait_ge(S["watt_in2"], 16)
            for k in range(KD):
                split_w(WO + k * D, D).then_inc(S["ow_split"], 1)
            dve.wait_ge(S["cst_in"], 16)
            v.tensor_copy(tri[:, :], cst[:, C_TRI:C_TRI + P]).then_inc(S["bf_ready"], 1)

            def kvm_out(b):
                dve.wait_ge(S["kvp_mm"], b + 1)
                if b >= 1:
                    dve.wait_ge(S["num_mm"], TB * b)
                for m in range(KD):
                    o = bank[4][:, m * (P + 1):(m + 1) * (P + 1)]
                    v.tensor_tensor(kvm[:, m, 0:P], o[:, 0:P], blk, ALU.mult)
                    last = v.tensor_scalar(kvm[:, m, P:P + HB], headm, o[:, P:P + 1], None, ALU.mult)
                last.then_inc(S["kvm_out"], 1)

            def o_out(b, t):
                dve.wait_ge(S["num_mm"], TB * b + t + 1)
                o = bank[5 + t % 2][:, 0:KD * (P + HB)].rearrange("p (k n) -> p k n", k=KD)
                zt = z[:, t % 2]
                link(v.tensor_scalar(zt, o[:, :, P:P + HB], cst[:, C_EPS + t:C_EPS + t + 1], None, ALU.add))
                link(v.reciprocal(zt, zt))
                if t == 0 and b >= 1:
                    dve.wait_ge(S["ot_mm"], b)
                for m in range(KD):
                    last = v.tensor_tensor(
                        o_sb[:, t, m * P:(m + 1) * P].rearrange("p (h e) -> p h e", h=HB),
                        o[:, m, 0:P].rearrange("p (h e) -> p h e", h=HB),
                        zt[:, m, :].unsqueeze(2).broadcast_to([P, HB, DH]), ALU.mult)
                last.then_inc(S["o_out"], 1)

            def ot_lo_out(b):
                if b >= 1:
                    dve.wait_ge(S["y_mm"], TB * b)
                for m in range(KD):
                    dve.wait_ge(S["ot_hi_out"], KD * b + m + 1)
                    v.tensor_tensor(ot_lo[:, m, :], bank[(4, 7)[m]][:, :], ot_hi[:, m, :].bitcast(F32),
                                    ALU.subtract).then_inc(S["ot_lo_out"], 1)

            def r_out(b, t):
                dve.wait_ge(S["y_mm"], TB * b + t + 1)
                if t == 0:
                    dve.wait_ge(S[f"res_in{b}"], 16)
                r = x1[:, b * TB + t, 0:D]
                v.tensor_tensor(r, bank[5 + t % 2][:, 0:D], r, ALU.add).then_inc(S["r_out"], 1)
                dve.wait_ge(S["r_out"], TB * b + t + 1)
                link(v.bn_stats(stat[:, t, :], r))
                return v.bn_aggr(mv[:, 0, t, :], stat[:, t, :])

            def moments(b):
                for t in range(TB):
                    last = r_out(b, t)
                last.then_inc(S["mom_out"], 1)

            def x1_norm(b):
                dve.wait_ge(S["mom_out"], b + 1)
                if b >= 1:
                    dve.wait_ge(S["x1_out"], TB * b)
                rstd(v, link, 0, fused=True).then_inc(S["nw_out"], 1)

            def top_two(b):
                dve.wait_ge(S["lg_mm"], b + 1)
                ts = slice(b * TB, (b + 1) * TB)
                v.tensor_copy(logit[:, ts, :], lg_bank.rearrange("p (t e) -> p t e", t=TB)
                              ).then_inc(S["lg_out"], 1)
                dve.wait_ge(S["lg_out"], b + 1)
                for t in range(b * TB, (b + 1) * TB):
                    link(v.max(top_v[:, t, :], logit[:, t, :]))
                    last = v.max_index(top_i[:, t, :], top_v[:, t, :], logit[:, t, :])
                link(last)

            def shared_h(b, c):
                i = b * CS + c
                dve.wait_ge(S["sg_out"], i + 1)
                if i >= 2:
                    dve.wait_ge(S["shh_out"], i - 1)
                    dve.wait_ge(S["shl_out"], i - 1)
                v.tensor_tensor(hf[:, i % 2, :], bank[2 * (i % 2) + 1][:, :], sg[:, i % 2, :], ALU.mult
                                ).then_inc(S["sh_out"], 1)

            def shared_lo(b, c):
                i = b * CS + c
                dve.wait_ge(S["shh_out"], i + 1)
                v.tensor_tensor(hh_lo[:, c, :], hf[:, i % 2, :], hh_hi[:, c, :].bitcast(F32), ALU.subtract
                                ).then_inc(S["shl_out"], 1)

            def shared_out(b):
                for t in range(TB):
                    if t % 2 == 0:
                        dve.wait_ge(S["sdn_mm"], 2 * b + t // 2 + 1)
                    r = x1[:, b * TB + t, 0:D]
                    if t == 0:
                        dve.wait_ge(S[f"scattered{b}"], 16 * TOPK * TB)
                    v.tensor_tensor(r, bank[5 + t // 2][:, (t % 2) * D:(t % 2 + 1) * D], r, ALU.add
                                    ).then_inc(S["sres_out"], 1)

            def route():
                link(v.tensor_copy(ix_f[:, :, :], top_i[:, :, 0:TOPK]))
                v.tensor_copy(x1[:, :, D], cst[:, C_TOK:C_TOK + T]).then_inc(S["tags_out"], 1)
                v.tensor_copy(x1[:, :, D + 1], ix_f[:, :, 0]).then_inc(S["tags_out"], 1)
                iota = cst[:, C_IOTA:C_IOTA + NE].unsqueeze(1).broadcast_to([P, T, NE])
                for j in range(TOPK):
                    link(v.tensor_tensor(hot[:, j, :].rearrange("p (t e) -> p t e", t=T), iota,
                                         ix_f[:, :, j:j + 1].broadcast_to([P, T, NE]), ALU.is_equal))
                v.tensor_tensor(hot_m[:, :], hot[:, 0, :], hot[:, 1, :], ALU.add).then_inc(S["hot_out"], 1)
                v.tensor_tensor(wtmp[:, 0, :], top_v[:, :, 1], top_v[:, :, 0], ALU.subtract).then_inc(S["tail_norm"], 1)

            def slots():
                c, ct, ci = cnt, cnt_i, None
                dve.wait_ge(S["rank_mm"], 1)
                link(v.tensor_scalar(ct[:, 0, :], bank[4][:, T * NE:(T + 1) * NE], float(P - 1), None, ALU.add))
                link(v.tensor_scalar(ct[:, 1, :], ct[:, 0, :], P.bit_length() - 1, None, ALU.logical_shift_right))
                link(v.tensor_copy(c[:, 0, :], ct[:, 1, :]))
                link(v.memset(c[:, 1, :], 1.0))
                link(v.tensor_tensor_scan(c[:, 2, :], c[:, 1, :], c[:, 0, :], 0.0, ALU.mult, ALU.add))
                link(v.tensor_tensor(c[:, 3, :], c[:, 2, :], c[:, 0, :], ALU.subtract))
                link(v.tensor_scalar(c[:, 4, :], c[:, 3, :], float(P), None, ALU.mult))
                link(v.tensor_tensor(pos[:, :].rearrange("p (t e) -> p t e", t=T),
                                     bank[4][:, 0:T * NE].rearrange("p (t e) -> p t e", t=T),
                                     c[:, 4, :].unsqueeze(1).broadcast_to([P, T, NE]), ALU.add))
                for j in range(TOPK):
                    link(v.tensor_tensor(hot[:, j, :], hot[:, j, :], pos[:, :], ALU.mult))
                    link(v.tensor_reduce(slot_f[:, j, :], hot[:, j, :].rearrange("p (t e) -> p t e", t=T), AX.X, ALU.add))
                v.tensor_copy(slot[:, :, :], slot_f[:, :, :]).then_inc(S["slots_out"], 1)
                link(v.tensor_tensor(te_c[:, :, :], c[:, 2, :].unsqueeze(1).broadcast_to([P, NTW, NE]),
                                     cst[:, C_TILE:C_TILE + NTW].unsqueeze(2).broadcast_to([P, NTW, NE]), ALU.is_le))
                link(v.tensor_reduce(te_f[:, :], te_c[:, :, :], AX.X, ALU.add))
                link(v.tensor_scalar(te_f[:, :], te_f[:, :], float(NE - 1), None, ALU.min))
                def column(n):
                    return te_f[0:1, :].rearrange("p (q w) -> p q w", w=RING)[:, n // RING:n // RING + WORDS, n % RING]
                link(v.tensor_copy(te_w[:, :], column(WORD_TILES - 1)))
                for n in reversed(range(WORD_TILES - 1)):
                    dst = te_w if n else te_i
                    ins = v.scalar_tensor_tensor(dst[:, :], te_w[:, :], float(1 << E_BITS), column(n), ALU.mult, ALU.add)
                    if n:
                        link(ins)
                ins.then_inc(S["te_out"], 1)
                dve.wait_ge(S["exp_out"], 1)
                link(v.tensor_scalar(wtmp[:, 2, :], wtmp[:, 1, :], 1.0, None, ALU.add))
                link(v.reciprocal(w_top[:, 0, :], wtmp[:, 2, :]))
                link(v.tensor_tensor(w_top[:, 1, :], wtmp[:, 1, :], w_top[:, 0, :], ALU.mult))

            for b in range(NB - 1):
                kvm_out(b)
                for t in range(TB):
                    o_out(b, t)
                    if b >= 1 and t == 1:
                        x1_norm(b - 1)
                if b >= 2:
                    top_two(b - 2)
                ot_lo_out(b)
                moments(b)
            b = NB - 1
            kvm_out(b)
            for t in range(TB):
                o_out(b, t)
                if t == 1:
                    x1_norm(b - 1)
            dve.wait_ge(S["xhi_ready"], NB)
            dve.wait_ge(S["q_mm"], KD * NB)
            dve.wait_ge(S["xlo_ready"], NB)
            top_two(b - 2)
            shared_h(0, 0)
            ot_lo_out(b)
            shared_h(0, 1)
            moments(b)
            x1_norm(b)
            top_two(b - 1)
            shared_lo(0, 0)
            shared_lo(0, 1)
            shared_h(0, 2)
            top_two(b)
            route()
            shared_lo(0, 2)
            shared_h(0, 3)
            shared_lo(0, 3)
            shared_h(1, 0)
            slots()
            shared_h(1, 1)
            for b in (1, 2):
                shared_lo(b, 0)
                shared_lo(b, 1)
                for c in (2, 3):
                    shared_h(b, c)
                    shared_lo(b, c)
                shared_out(b - 1)
                if b < 2:
                    shared_h(b + 1, 0)
                    shared_h(b + 1, 1)
            shared_out(2)
            def e_x_lo(j, u, first=False):
                dve.wait_ge(S["xe_hi_out"], j + 1)
                if not first:
                    dve.wait_ge(S["egu_mm"], j - 1)
                v.tensor_tensor(xe_lo[:, u % 2, :, :],
                                bank[(4, 7)[u % 2]][:, 0:KD * P].rearrange("p (k n) -> p k n", k=KD),
                                xe_hi[:, u % 2, :, :].bitcast(F32), ALU.subtract).then_inc(S["xe_lo_out"], 1)

            def e_h(j, u, first=False):
                dve.wait_ge(S["eg_out"], j + 1)
                if not first:
                    dve.wait_ge(S["eht_mm"], j - 1)
                v.tensor_tensor(eh[:, u % 2, :], bank[u % 2][:, IM:2 * IM], eg[:, u % 2, :], ALU.mult
                                ).then_inc(S["eh_out"], 1)

            def e_h_lo(j, u, first=False):
                dve.wait_ge(S["he_hi_out"], j + 1)
                if not first:
                    dve.wait_ge(S["ey_mm"], j - 1)
                v.tensor_tensor(he_lo[:, u % 2, :], bank[2 + u % 2][:, 0:P], he_hi[:, u % 2, :].bitcast(F32),
                                ALU.subtract).then_inc(S["he_lo_out"], 1)

            e_x_lo(0, 0, first=True)
            e_x_lo(1, 1, first=True)
            e_h(0, 0, first=True)
            e_x_lo(2, 2)
            e_h(1, 1, first=True)
            e_h_lo(0, 0, first=True)
            e_x_lo(3, 3)
            e_h(2, 2)
            e_h_lo(1, 1, first=True)
            for n in range(TAG_LOADS):
                j = slice(n * NT // TAG_LOADS, (n + 1) * NT // TAG_LOADS)
                dve.wait_ge(tag_in[n], 16)
                link(v.tensor_tensor(dst_f[:, j], tag[:, j, 1], te_f[:, j.start + RING - 1:j.stop + RING - 1], ALU.not_equal))
                v.tensor_tensor(dst[:, j], dst_f[:, j], tag[:, j, 0], ALU.add).then_inc(S["dst_out"], 1)
            with dve.Fori(0, NT // RING - 1) as i:
                for w in range(RING):
                    s = i * RING + (w + 2)
                    e_x_lo(s + 2, w)
                    e_h(s + 1, (w + 3) % RING)
                    e_h_lo(s, (w + 2) % RING)
            e_h(NT - 1, (NT - 1) % RING)
            for s in (NT - 2, NT - 1):
                e_h_lo(s, s % RING)

            def combine(n):
                dve.wait_ge(pair_in[n], 16)
                tiles = range(n * UNIT, (n + 1) * UNIT)
                dve.wait_ge(S["sres_out"], tiles[-1] + 1)
                y = pair[n % PAIRS]
                link(*(v.scalar_tensor_tensor(x1[:, i, 0:D], y[:, i % UNIT, 0, :], w_top[:, 0, i:i + 1],
                                              x1[:, i, 0:D], ALU.mult, ALU.add) for i in tiles))
                for i in tiles:
                    v.scalar_tensor_tensor(x1[:, i, 0:D], y[:, i % UNIT, 1, :], w_top[:, 1, i:i + 1],
                                           x1[:, i, 0:D], ALU.mult, ALU.add).then_inc(S["acc_out"], 1)
                for i in tiles:
                    dve.wait_ge(S["acc_out"], i + 1)
                    ins = v.bn_stats(stat[:, i % TB, :], x1[:, i, 0:D])
                    if i == tiles[-1]:
                        link(ins)
                    else:
                        ins.then_inc(S["stat_out"], 1)
                dve.wait_ge(S["stat_out"], n + 1)
                b = tiles[0] // TB
                if b >= 2:
                    dve.wait_ge(S["ln_out"], b - 1)
                for i in tiles:
                    v.bn_aggr(mv[:, b % 2, i % TB, :], stat[:, i % TB, :]).then_inc(S["bn_out"], 1)

            units = iter(range(T // UNIT))
            for c in range(CS):
                shared_h(3, c)
                shared_lo(3, c)
                if c >= 1:
                    combine(next(units))
            for n in range(CS - 1, T // UNIT - UNIT):
                combine(next(units))
            shared_out(3)
            for n in units:
                combine(n)
            dve.wait_ge(S["bn_out"], T)
            dve.wait_ge(S["fin_out"], TB * (NB - 2))
            rstd(v, link, (NB - 1) % 2, fused=True).then_inc(S["ln_last_out"], 1)

        @block.gpsimd
        def _(pool):
            g = nc.gpsimd
            g.memset(fill[:, 0:D], 0.0).then_inc(S["pool_chain"], 1)
            pool.wait_ge(S["cst_in"], 16)
            g.tensor_copy(fill[:, D:DT], cst[:, C_FILL:C_FILL + TAG]).then_inc(S["pool_chain"], 1)
            pool.wait_ge(S["pool_chain"], 2)
            pool.sem_inc(S["fill_made"], 1)

            def split_x_lo(b):
                pool.wait_ge(S["xhi_ready"], b + 1)
                for k in range(KD):
                    last = g.tensor_tensor(xt_lo[:, b % 2, k, :], xt_raw[:, b % 2, k, :],
                                           xt_hi[:, b % 2, k, :].bitcast(F32), ALU.subtract)
                last.then_inc(S["xlo_ready"], 1)

            def split_chunk(i):
                pool.wait_ge(stage_in[i % 2], 16 * (i // 2 + 1))
                c = slice(i * CHUNK, (i + 1) * CHUNK)
                g.tensor_copy(wf_hi[:, c], stage[:, i % 2, :]).then_inc(S["wf_split"], 1)
                pool.wait_ge(S["wf_split"], 2 * i + 1)
                g.tensor_tensor(wf_lo[:, c], stage[:, i % 2, :], wf_hi[:, c].bitcast(F32), ALU.subtract
                                ).then_inc(S["wf_split"], 1)

            def x1_lo(b):
                pool.wait_ge(S["x1hi_out"], KD * (b + 1))
                for m in range(KD):
                    g.tensor_tensor(x1t_lo[:, b, m, :], x1_t[:, m, :], x1t_hi[:, b, m, :].bitcast(F32),
                                    ALU.subtract).then_inc(S["x1lo_out"], 1)

            per = -(-NCH // NB)
            split_x_lo(1)
            done = 0
            for b in range(NB):
                for n in range(per):
                    if done < NCH:
                        split_chunk(done)
                        done += 1
                    if n == 1 and b + 2 < NB:
                        split_x_lo(b + 2)
                    if n == 3 and b >= 1:
                        x1_lo(b - 1)
            x1_lo(NB - 1)

            pool.wait_ge(S["zero_in"], 16 * FILLS)
            pool.wait_ge(S["slots_out"], 1)
            pool.wait_ge(S["tags_out"], 2)
            pool.wait_ge(S["x1_out"], T)
            for t in range(T):
                for j in range(TOPK):
                    pool.indirect_dma_start(out=x_scat, out_offset=bass.IndirectOffsetOnAxis(ap=slot[:, j, t:t + 1], axis=0),
                                            in_=x1[:, t, :], in_offset=None).then_inc(S[f"scattered{t // TB}"], 16)
            def send(j, u):
                pool.wait_ge(S["ey_out"], j + 1)
                pool.indirect_dma_start(out=y_scat, out_offset=bass.IndirectOffsetOnAxis(ap=dst[:, j:j + 1], axis=0),
                                        in_=ey[:, u, :], in_offset=None,
                                        bounds_check=2 * TOK - 1, oob_is_err=False).then_inc(ey_st[u], 16)

            for j in range(NT):
                if j % (NT // TAG_LOADS) == 0:
                    pool.wait_ge(S["dst_out"], j // (NT // TAG_LOADS) + 1)
                send(j, j % RING)

            chain = [2]

            def link(ins):
                chain[0] += 1
                ins.then_inc(S["pool_chain"], 1)
                pool.wait_ge(S["pool_chain"], chain[0])

            for b in range(NB - 1):
                pool.wait_ge(S["bn_out"], TB * (b + 1))
                if b >= 2:
                    pool.wait_ge(S["fin_out"], TB * (b - 1))
                rstd(g, link, b % 2, fused=False).then_inc(S["ln_out"], 1)


def constants():
    p = np.arange(P)
    c = np.zeros((P, NC_), np.float32)
    c[:, C_ID:C_ID + P] = np.eye(P)
    c[:, C_BLK:C_BLK + P] = p[:, None] // DH == p[None, :] // DH
    c[:, C_HEAD:C_HEAD + HB] = p[:, None] // DH == np.arange(HB)[None, :]
    decay = np.exp(-(np.arange(TB)[None, :] * P + p[:, None]).astype(np.float32) / np.float32(SEQ))
    c[:, C_DEC:C_DEC + TB] = decay
    c[:, C_EPS:C_EPS + TB] = np.float32(EPS_ATT) / decay
    c[:, C_IOTA:C_IOTA + NE] = np.arange(NE)
    c[:, C_TRI:C_TRI + P] = p[:, None] < p[None, :]
    c[:, C_TILE:C_TILE + NTW] = np.arange(NTW) - (RING - 1)
    c[:, C_TOK:C_TOK + T] = 2 * (np.arange(T)[None, :] * P + p[:, None])
    c[:, C_FILL:C_FILL + TAG] = np.stack([2 * (TOK + p), -np.ones(P)], axis=1)
    return c


def rows(w):
    return w.reshape(-1, P, w.shape[-1]).transpose(1, 0, 2).reshape(P, -1)


def kernel(**inputs):
    import concourse.bacc as bacc
    from concourse.bass_utils import run_bass_kernel_spmd

    a = {n.replace("L0_", ""): np.asarray(v) for n, v in inputs.items()}
    x = a["attn_x"]
    wkv = np.concatenate([a["attn_Wk"].T, a["attn_Wv"].T], axis=1)
    gu, dn = a["ffn_w_gate_up"], a["ffn_w_down"]
    arrays = {
        "xT": np.stack([rows(x[b].T) for b in range(NB)]),
        "x": x,
        "watt": np.concatenate([rows(wkv), rows(a["attn_Wq"].T), rows(a["attn_Wo"].T)], axis=1),
        "batt": np.concatenate([a["attn_bk"], a["attn_bv"], a["attn_bo"]])[None, :],
        "bq": rows(a["attn_bq"][:, None]),
        "wffn": np.concatenate([rows(a["ffn_w_sh_gate_up"]), rows(a["ffn_w_sh_down"])]
                               + [rows(w[e]) for e in range(NE) for w in (gu, dn)], axis=1),
        "wgate": rows(a["ffn_w_gate"]).reshape(P, KD, NE),
        "consts": constants(),
    }
    arrays = {n: np.ascontiguousarray(v) for n, v in arrays.items()}
    nc = bacc.Bacc("TRN2", target_bir_lowering=False, num_devices=1)
    aps = [nc.dram_tensor(f"in_{n}", v.shape, mybir.dt.from_np(v.dtype), kind="ExternalInput").ap()
           for n, v in arrays.items()]
    out = nc.dram_tensor("out_0", [NB, SEQ, D], F32, kind="ExternalOutput").ap()
    build(nc, *aps, out)
    r = run_bass_kernel_spmd(nc, [{f"in_{n}": v for n, v in arrays.items()}], core_ids=[0])
    return r.results[0]["out_0"]
```

```python
from contextlib import ExitStack

import numpy as np

import concourse.bass as bass
from concourse import mybir

F32 = mybir.dt.float32
F32R = mybir.dt.float32r
BF16 = mybir.dt.bfloat16
I32 = mybir.dt.int32
U32 = mybir.dt.uint32
ALU = mybir.AluOpType
ACT = mybir.ActivationFunctionType
AX = mybir.AxisListType

P = 128
NB, SEQ, D = 4, 512, 256
KD = D // P
NH, DH = 16, 16
HB = P // DH
NE, TOPK, IM, IS = 8, 2, 128, 512
CS = IS // P
TB = SEQ // P
T = NB * TB
TOK = NB * SEQ
NT = -(-((TOK * TOPK + NE * (P - 1)) // P) // 4) * 4
NSLOT = NT * P
EPS_ATT, EPS_LN = 1e-6, 1e-5
AW = KD * 2 * D + KD * D + KD * D
WKV, WQ, WO = 0, KD * 2 * D, KD * 2 * D + KD * D
SH_GU = 0
SH_DN = SH_GU + KD * 2 * IS
EX = SH_DN + CS * D
EX_W = KD * 2 * IM + D
FW = EX + NE * EX_W
CHUNK = 512
NCH = FW // CHUNK
TAG = 2
DT = D + TAG
FILLS = 5
UNIT = 2
ALONE = 1
LATE = (T - TB) // UNIT
LAST_ACT = 1
RING = 4
WORDS = NT // RING + 1
WORD_TILES = RING + 2
NTW = (WORDS + 1) * RING
E_BITS = (NE - 1).bit_length()
C_ID, C_BLK = 0, P
C_HEAD = C_BLK + P
C_DEC = C_HEAD + HB
C_EPS = C_DEC + TB
C_IOTA = C_EPS + TB
C_TRI = C_IOTA + NE
C_TILE = C_TRI + P
C_TOK = C_TILE + NTW
C_FILL = C_TOK + T
NC_ = C_FILL + TAG
RSQRT_MAGIC = 0x5F3759DF


def build(nc, xT, x, watt, batt, bq, wffn, wgate, consts, out):
    x_scat = nc.dram_tensor("x_slots", [NSLOT, DT], F32).ap()
    y_scat = nc.dram_tensor("y_pairs", [2 * TOK, D], F32).ap()
    ctx = ExitStack()
    with ctx:
        def sb(name, shape, dt=F32):
            return ctx.enter_context(nc.sbuf_tensor(name, shape, dt))

        def sem(name):
            return ctx.enter_context(nc.semaphore(name))

        cst = sb("cst", [P, NC_])
        tri = sb("tri", [P, P], BF16)
        ones = sb("ones", [P, P], BF16)
        one_f = sb("one_f", [33, P], F32R)
        b_row = sb("b_row", [33, 3 * D], F32R)
        bq_sb = sb("bq_sb", [P, KD])
        wg_sb = sb("wg_sb", [P, KD, NE])
        wa_hi = sb("wa_hi", [P, AW], F32R)
        wa_lo = sb("wa_lo", [P, AW], F32R)
        wf_hi = sb("wf_hi", [P, FW], F32R)
        wf_lo = sb("wf_lo", [P, FW], F32R)
        stage = sb("stage", [P, 2, CHUNK])
        xt_raw = sb("xt_raw", [P, 2, KD, SEQ])
        xt_hi = sb("xt_hi", [P, 2, KD, SEQ], F32R)
        xt_lo = sb("xt_lo", [P, 2, KD, SEQ], F32R)
        x1 = sb("x1", [P, T, DT])
        wa_raw = x1[:, T // 2:, :].rearrange("p t d -> p (t d)")[:, 0:AW]
        k_sb = sb("k_sb", [P, TB, D])
        v_sb = sb("v_sb", [P, TB, KD, P + 1])
        q_t = sb("q_t", [P, KD, SEQ])
        kvm = sb("kvm", [P, KD, P + HB])
        z = sb("z", [P, 2, KD, HB])
        o_sb = sb("o_sb", [P, TB, D])
        ot_hi = sb("ot_hi", [P, KD, SEQ], F32R)
        ot_lo = sb("ot_lo", [P, KD, SEQ], F32R)
        x1_t = sb("x1_t", [P, KD, SEQ])
        x1t_hi = sb("x1t_hi", [P, NB, KD, SEQ], F32R)
        x1t_lo = sb("x1t_lo", [P, NB, KD, SEQ], F32R)
        warm = sb("warm", [P, 2])
        stat = sb("stat", [P, TB, 6])
        mv = sb("mv", [P, NB, TB, 2])
        nw = sb("nw", [P, NB, 4, TB])
        logit = sb("logit", [P, T, NE])
        top_v = sb("top_v", [P, T, 8])
        top_i = sb("top_i", [P, T, 8], U32)
        ix_f = sb("ix_f", [P, T, TOPK])
        hot = sb("hot", [P, TOPK, T * NE])
        hot_m = sb("hot_m", [P, T * NE], BF16)
        pos = sb("pos", [P, T * NE])
        slot_f = sb("slot_f", [P, TOPK, T])
        slot = sb("slot", [P, TOPK, T], U32)
        w_top = sb("w_top", [P, TOPK, T])
        wtmp = sb("wtmp", [P, 3, T])
        cnt = sb("cnt", [P, 6, NE])
        cnt_i = sb("cnt_i", [P, 2, NE], I32)
        te_c = k_sb[:, 0:2, :].rearrange("p a d -> p (a d)")[:, 0:NTW * NE].rearrange("p (t e) -> p t e", e=NE)
        te_f = sb("te_f", [P, NTW])
        tag = sb("tag", [P, NT, TAG])
        dst_f = sb("dst_f", [P, NT])
        dst = sb("dst", [P, NT], U32)
        te_w = sb("te_w", [1, WORDS])
        te_i = sb("te_i", [1, WORDS], I32)
        b_raw = k_sb[0:33, 0:3, :].rearrange("p a d -> p (a d)")
        fill = x1_t[:, 0, 0:DT]
        sg, hf = xt_raw[:, 0], xt_raw[:, 1]
        hh_hi = xt_hi[:, :, :, :].rearrange("p a k n -> p (a k) n")
        hh_lo = xt_lo[:, :, :, :].rearrange("p a k n -> p (a k) n")
        xg = o_sb
        ey = x1_t[:, :, :].rearrange("p k (a n) -> p (k a) n", a=2)
        xe_hi, xe_lo = (o[:, 0, :].rearrange("p (a k n) -> p a k n", a=2, k=KD) for o in (ot_hi, ot_lo))
        he_hi, he_lo = (o[:, 1, 0:2 * IM].rearrange("p (a n) -> p a n", a=2) for o in (ot_hi, ot_lo))
        eg = q_t[:, 0, 0:2 * IM].rearrange("p (a n) -> p a n", a=2)
        eh = q_t[:, 1, 0:2 * IM].rearrange("p (a n) -> p a n", a=2)
        pair = [k_sb[:, :, :].rearrange("p t d -> p (t d)"),
                v_sb[:, :, :, :].rearrange("p t k n -> p (t k n)")[:, 0:2 * UNIT * D],
                o_sb[:, :, :].rearrange("p t d -> p (t d)"),
                x1_t[:, :, :].rearrange("p k n -> p (k n)"),
                q_t[:, :, :].rearrange("p k n -> p (k n)"),
                stage[:, :, :].rearrange("p a n -> p (a n)")]
        n_pair = len(pair)
        pair = [o.rearrange("p (i j d) -> p i j d", i=UNIT, j=TOPK) for o in pair]

        ident = cst[:, C_ID:C_ID + P]
        blk = cst[:, C_BLK:C_BLK + P]
        headm = cst[:, C_HEAD:C_HEAD + HB]

        bank = [ctx.enter_context(nc.psum_tensor(f"bank{i}", [P, 512], F32)) for i in range(8)]

        lg_bank = bank[7][:, 0:TB * NE]

        def shared_sum(t):
            return bank[5 + t // 2][:, (t % 2) * D:(t % 2 + 1) * D]

        def shared_sums(t):
            return bank[5 + t // 2][:, :].rearrange("p (i d) -> p i d", i=2)

        def x1t_bank(b, m):
            return bank[(4, 6)[m]] if b == NB - 1 else bank[2 + m]

        names = """
            b_cleared ones_ready bf_ready bias_in bias_ready cst_in small_in
            watt_in0 watt_in0b watt_in1 watt_in2 kvw_split qw_split ow_split
            xt_half_in xt_in0 xt_in1 xhi_half_out xlo_half_out xhi_ready xlo_ready
            res_in0 res_in1 res_in2 res_in3 stage_in0 stage_in1 wf_split fill_made zero_in
            kv_mm kv_out q_mm q_out kvp_mm kvm_out num_mm o_out ot_mm ot_hi_out ot_lo_out
            y_mm r_out st_out mom_out nw_out nw_pool_out nw_last_out x1_out
            x1t_mm x1f_out x1hi_out x1lo_out lg_mm lg_out
            hot_out gap_out exp_out wtop_out tags_out rank_mm slots_out te_out
            scattered0 scattered1 scattered2 scattered3
            sgu_mm sg_out sh_out shh_out shl_out sdn_mm sres_out sum_mm
            tag_in dst_out xt_e_mm xe_hi_out xe_lo_out egu_mm eg_out eh_out
            eht_mm he_hi_out he_lo_out ey_mm ey_out
            wy_out add_out acc_out stat_out bn_out ln_out ln_last_out fin_out fin_last_out stored
            dve_chain pool_chain""".split()
        S = {n: sem(n) for n in names}
        xg_in = [sem(f"xg_in{u}") for u in range(RING)]
        ey_st = [sem(f"ey_st{u}") for u in range(RING)]
        pair_in = [sem(f"pair_in{n}") for n in range(T // UNIT)]
        xt_in = [S["xt_in0"], S["xt_in1"]]
        stage_in = [S["stage_in0"], S["stage_in1"]]

        def rstd(v, link, h, fused):
            va, y, t, m = (nw[:, h, n, :] for n in range(4))
            link(v.tensor_scalar(va, mv[:, h, :, 1], EPS_LN, None, ALU.add))
            link(v.tensor_scalar(y.bitcast(I32), va.bitcast(I32), -0.5, float(RSQRT_MAGIC), ALU.mult, ALU.add))
            for _ in range(3):
                if fused:
                    link(v.scalar_tensor_tensor(t, y, -0.5, y, ALU.mult, ALU.mult))
                    link(v.tensor_tensor(t, t, va, ALU.mult))
                    link(v.scalar_tensor_tensor(y, t, 1.5, y, ALU.add, ALU.mult))
                else:
                    link(v.tensor_tensor(t, y, y, ALU.mult))
                    link(v.tensor_tensor(t, t, va, ALU.mult))
                    link(v.tensor_scalar(t, t, -0.5, 1.5, ALU.mult, ALU.add))
                    link(v.tensor_tensor(y, t, y, ALU.mult))
            if fused:
                return v.scalar_tensor_tensor(m, mv[:, h, :, 0], -1.0, y, ALU.mult, ALU.mult)
            link(v.tensor_tensor(m, mv[:, h, :, 0], y, ALU.mult))
            return v.tensor_scalar(m, m, -1.0, None, ALU.mult)

        block = ctx.enter_context(nc.Block())

        @block.sync
        def _(sp):
            def load_xt(b):
                sp.dma_start(xt_raw[:, b % 2], xT[b].rearrange("p (k n) -> p k n", k=KD)).then_inc(xt_in[b % 2], 16)

            def load_res(b):
                sp.dma_start(x1[:, b * TB:(b + 1) * TB, 0:D], x[b].rearrange("(t p) d -> p t d", p=P)
                             ).then_inc(S[f"res_in{b}"], 16)

            HS = SEQ // 2
            for h, into in enumerate((S["xt_half_in"], xt_in[0])):
                sp.dma_start(xt_raw[:, 0, :, h * HS:(h + 1) * HS],
                             xT[0].rearrange("p (k n) -> p k n", k=KD)[:, :, h * HS:(h + 1) * HS]).then_inc(into, 16)
                if h == 0:
                    for k in range(KD):
                        w = slice(WKV + k * 2 * D, WKV + (k + 1) * 2 * D)
                        sp.dma_start(wa_raw[:, w], watt[:, w]).then_inc(S["watt_in0" if k == 0 else "watt_in0b"], 16)
            sp.dma_start(cst[:, :], consts).then_inc(S["cst_in"], 16)
            sp.dma_start(wa_raw[:, WQ:WO], watt[:, WQ:WO]).then_inc(S["watt_in1"], 16)
            sp.dma_start(bq_sb[:, :], bq).then_inc(S["small_in"], 16)
            sp.dma_start(wg_sb[:, :, :], wgate).then_inc(S["small_in"], 16)
            load_xt(1)
            sp.dma_start(wa_raw[:, WO:AW], watt[:, WO:AW]).then_inc(S["watt_in2"], 16)
            load_res(0)
            load_res(1)

            def load_chunk(i):
                if i >= 2:
                    sp.wait_ge(S["wf_split"], 2 * (i - 1))
                sp.dma_start(stage[:, i % 2, :], wffn[:, i * CHUNK:(i + 1) * CHUNK]).then_inc(stage_in[i % 2], 16)

            for i in range(NCH):
                if i < FILLS:
                    if i == 0:
                        sp.wait_ge(S["fill_made"], 1)
                    n = NT // FILLS
                    sp.dma_start(x_scat[i * n * P:(i + 1) * n * P, :].rearrange("(a p) d -> p a d", p=P),
                                 fill.unsqueeze(1).broadcast_to([P, n, DT])).then_inc(S["zero_in"], 16)
                if i == 6:
                    sp.wait_ge(S["ow_split"], 2)
                    load_res(2)
                    load_res(3)
                if i in (2, 6):
                    b = 2 if i == 2 else 3
                    sp.wait_ge(S["xhi_ready"], b - 1)
                    sp.wait_ge(S["xlo_ready"], b - 1)
                    load_xt(b)
                load_chunk(i)

            for b in range(NB):
                sp.wait_ge(S[f"scattered{b}"], 16 * TOPK * TB)

            def load_tile(j, u, first=False):
                if not first:
                    sp.wait_ge(S["xt_e_mm"], j - RING + 1)
                sp.dma_start(xg[:, u, :], x_scat[bass.ds(j * P, P), 0:D]).then_inc(xg_in[u], 16)

            for u in range(RING):
                load_tile(u, u, first=True)
            sp.dma_start(tag[:, :, :], x_scat.rearrange("(t p) d -> p t d", p=P)[:, :, D:DT]).then_inc(S["tag_in"], 16)
            with sp.Fori(0, NT // RING - 1) as i:
                for v in range(RING):
                    load_tile(i * RING + (RING + v), v)

            for u in range(RING):
                sp.wait_ge(ey_st[u], 16 * (NT // RING))
            for n in range(T // UNIT):
                if n >= n_pair:
                    sp.wait_ge(S["acc_out"], UNIT * (n - n_pair + 1))
                rows = slice(2 * n * UNIT * P, 2 * (n + 1) * UNIT * P)
                sp.dma_start(pair[n % n_pair].rearrange("p i j d -> p i (j d)"),
                             y_scat[rows, :].rearrange("(i p j) d -> p i (j d)", p=P, j=TOPK)).then_inc(pair_in[n], 16)
            for n in range(T // UNIT):
                done = (n + 1) * UNIT - (T - TB)
                if done <= 0:
                    sp.wait_ge(S["fin_out"], (n + 1) * UNIT)
                else:
                    sp.wait_ge(S["fin_last_out"], min(done, TB - LAST_ACT))
                    if done > TB - LAST_ACT:
                        sp.wait_ge(S["fin_out"], T - TB + done - (TB - LAST_ACT))
                b, t = divmod(n * UNIT, TB)
                sp.dma_start(out[b].rearrange("(t p) d -> p t d", p=P)[:, t:t + UNIT, :],
                             x1[:, n * UNIT:(n + 1) * UNIT, 0:D]).then_inc(S["stored"], 16)
            sp.wait_ge(S["stored"], 16 * (T // UNIT))

        @block.tensor
        def _(pe):
            mm = nc.tensor.matmul

            def split3(o, w_hi, w_lo, m_hi, m_lo, start, stop, **more):
                mm(o, w_hi, m_hi, start=start, stop=False, **more)
                mm(o, w_hi, m_lo, start=False, stop=False, **more)
                return mm(o, w_lo, m_hi, start=False, stop=stop, **more)

            def proj_kv(b, t):
                i = b * TB + t
                if t == 0 and b >= 1:
                    pe.wait_ge(S["xhi_ready"], b + 1)
                    pe.wait_ge(S["xlo_ready"], b + 1)
                if i >= 2:
                    pe.wait_ge(S["kv_out"], i - 1)
                o = bank[t % 2][:, :]
                for k in range(KD):
                    if i == 0:
                        pe.wait_ge(S["kvw_split"], k + 1)
                    c = slice(t * P, (t + 1) * P)
                    w = slice(WKV + k * 2 * D, WKV + (k + 1) * 2 * D)
                    split3(o, xt_hi[:, b % 2, k, c], xt_lo[:, b % 2, k, c], wa_hi[:, w], wa_lo[:, w], k == 0, False)
                if i == 0:
                    pe.wait_ge(S["ones_ready"], 2)
                    pe.wait_ge(S["bias_ready"], 1)
                mm(o, one_f[:, :], b_row[:, 0:2 * D], start=False, stop=True).then_inc(S["kv_mm"], 1)

            def proj_q(b, ms=range(KD)):
                if b == 0:
                    pe.wait_ge(S["qw_split"], 2)
                for m in ms:
                    if b >= 1:
                        pe.wait_ge(S["q_out"], KD * (b - 1) + m + 1)
                    if b >= 3:
                        pe.wait_ge(S["x1f_out"], KD * (b - 3) + m + 1)
                    o = bank[2 + m][:, :]
                    for k in range(KD):
                        w = slice(WQ + k * D + m * P, WQ + k * D + (m + 1) * P)
                        last = split3(o, wa_hi[:, w], wa_lo[:, w], xt_hi[:, b % 2, k, :], xt_lo[:, b % 2, k, :],
                                      k == 0, k == KD - 1)
                    last.then_inc(S["q_mm"], 1)

            def k_t_v(b):
                pe.wait_ge(S["kv_out"], TB * (b + 1))
                if b >= 1:
                    pe.wait_ge(S["ot_hi_out"], KD * (b - 1) + 1)
                    pe.wait_ge(S["ot_lo_out"], KD * (b - 1) + 1)
                for m in range(KD):
                    o = bank[4][:, m * (P + 1):(m + 1) * (P + 1)]
                    for t in range(TB):
                        last = mm(o, k_sb[:, t, m * P:(m + 1) * P], v_sb[:, t, m, :],
                                  start=(t == 0), stop=(t == TB - 1))
                last.then_inc(S["kvp_mm"], 1)

            def attend(b, ts):
                pe.wait_ge(S["kvm_out"], b + 1)
                pe.wait_ge(S["q_out"], KD * (b + 1))
                for t in ts:
                    if t >= 2:
                        pe.wait_ge(S["o_out"], TB * b + t - 1)
                    elif b >= 1:
                        pe.wait_ge(S["r_out"], TB * b)
                    o = bank[5 + t % 2]
                    for m in range(KD):
                        last = mm(o[:, m * (P + HB):(m + 1) * (P + HB)], q_t[:, m, t * P:(t + 1) * P], kvm[:, m, :],
                                  start=True, stop=True)
                    last.then_inc(S["num_mm"], 1)

            def o_transposed(b):
                if b >= 1:
                    pe.wait_ge(S["ot_lo_out"], KD * b)
                if b >= 2:
                    pe.wait_ge(S["lg_out"], b - 1)
                for t in range(TB):
                    pe.wait_ge(S["o_out"], TB * b + t + 1)
                    for m in range(KD):
                        last = nc.tensor.transpose(bank[(4, 7)[m]][:, t * P:(t + 1) * P],
                                                   o_sb[:, t, m * P:(m + 1) * P], ident)
                last.then_inc(S["ot_mm"], 1)

            def proj_o(b):
                pe.wait_ge(S["ot_hi_out"], KD * (b + 1))
                pe.wait_ge(S["ot_lo_out"], KD * (b + 1))
                if b == 0:
                    pe.wait_ge(S["ow_split"], 2)
                for t in range(TB):
                    if t >= 2:
                        pe.wait_ge(S["r_out"], TB * b + t - 1)
                    o = bank[5 + t % 2][:, 0:D]
                    mm(o, one_f[:, :], b_row[:, 2 * D:3 * D], start=True, stop=False)
                    for k in range(KD):
                        c = slice(t * P, (t + 1) * P)
                        w = slice(WO + k * D, WO + (k + 1) * D)
                        last = split3(o, ot_hi[:, k, c], ot_lo[:, k, c], wa_hi[:, w], wa_lo[:, w], False, k == KD - 1)
                    last.then_inc(S["y_mm"], 1)

            def x1_transposed(b):
                pe.wait_ge(S["x1_out"], TB * (b + 1))
                if b < NB - 2:
                    pe.wait_ge(S["q_out"], KD * (b + 3))
                for t in range(TB):
                    for m in range(KD):
                        last = nc.tensor.transpose(x1t_bank(b, m)[:, t * P:(t + 1) * P],
                                                   x1[:, b * TB + t, m * P:(m + 1) * P], ident)
                last.then_inc(S["x1t_mm"], 1)

            def router(b):
                pe.wait_ge(S["x1f_out"], KD * (b + 1))
                pe.wait_ge(S["ot_lo_out"], KD * min(b + 2, NB))
                if b >= 1:
                    pe.wait_ge(S["lg_out"], b)
                for t in range(TB):
                    for k in range(KD):
                        last = mm(lg_bank[:, t * NE:(t + 1) * NE], x1_t[:, k, t * P:(t + 1) * P], wg_sb[:, k, :],
                                  start=(k == 0), stop=(k == KD - 1))
                last.then_inc(S["lg_mm"], 1)

            def ranks():
                pe.wait_ge(S["hot_out"], 1)
                o = bank[4][:, 0:(T + 1) * NE]
                mm(o[:, 0:T * NE], tri[:, :], hot_m[:, :], start=True, stop=False, skip_group_check=True)
                for s in range(1, T + 1):
                    last = mm(o[:, s * NE:], ones[:, :], hot_m[:, 0:(T + 1 - s) * NE], start=False, stop=(s == T),
                              skip_group_check=True)
                last.then_inc(S["rank_mm"], 1)

            def shared_gu(b, c, part=None):
                i = b * CS + c
                if c == 0:
                    pe.wait_ge(S["x1hi_out"], KD * (b + 1))
                    pe.wait_ge(S["x1lo_out"], KD * (b + 1))
                if i >= 2:
                    pe.wait_ge(S["sh_out"], i - 1)
                for g in range(2) if part is None else (part,):
                    o = bank[2 * (i % 2) + g][:, :]
                    for k in range(KD):
                        w = slice(SH_GU + k * 2 * IS + g * IS + c * P, SH_GU + k * 2 * IS + g * IS + (c + 1) * P)
                        last = split3(o, wf_hi[:, w], wf_lo[:, w], x1t_hi[:, b, k, :], x1t_lo[:, b, k, :],
                                      k == 0, k == KD - 1)
                if part != 0:
                    last.then_inc(S["sgu_mm"], 1)

            def shared_dn(b):
                pe.wait_ge(S["shh_out"], CS * (b + 1))
                pe.wait_ge(S["shl_out"], CS * (b + 1))
                for t in range(TB):
                    if b >= 1:
                        pe.wait_ge(S["sres_out"], TB * (b - 1) + 2 * (t // 2) + 2)
                    o = shared_sum(t)
                    if b == NB - 1 and t % 2 == 0:
                        mm(shared_sums(t), ident, x1[:, b * TB + t:b * TB + t + 2, 0:D], start=True, stop=False,
                           skip_group_check=True)
                    for c in range(CS):
                        w = slice(SH_DN + c * D, SH_DN + (c + 1) * D)
                        n = slice(t * P, (t + 1) * P)
                        if b < NB - 1:
                            last = split3(o, hh_hi[:, c, n], hh_lo[:, c, n], wf_hi[:, w], wf_lo[:, w],
                                          c == 0, c == CS - 1)
                        else:
                            last = split3(o, hh_hi[:, c, n], hh_lo[:, c, n], wf_hi[:, w], wf_lo[:, w],
                                          False, False, skip_group_check=True)
                    if t % 2 and b < NB - 1:
                        last.then_inc(S["sdn_mm"], 1)

            for t in range(TB):
                if t == 0:
                    pe.wait_ge(S["xhi_half_out"], 1)
                    pe.wait_ge(S["xlo_half_out"], 1)
                if t == TB // 2:
                    pe.wait_ge(S["xhi_ready"], 1)
                    pe.wait_ge(S["xlo_ready"], 1)
                proj_kv(0, t)
            proj_q(0)
            pe.wait_ge(S["cst_in"], 16)
            pe.wait_ge(S["small_in"], 32)
            for b in range(NB):
                more = b + 1 < NB
                k_t_v(b)
                if more:
                    proj_kv(b + 1, 0)
                    proj_kv(b + 1, 1)
                    attend(b, range(0, 2))
                    proj_kv(b + 1, 2)
                    proj_kv(b + 1, 3)
                    attend(b, range(2, TB))
                    proj_q(b + 1, [0])
                    if b == 0:
                        o_transposed(b)
                        proj_q(b + 1, [1])
                    else:
                        proj_q(b + 1, [1])
                        o_transposed(b)
                        x1_transposed(b - 1)
                    proj_o(b)
                else:
                    pe.wait_ge(S["kv_out"], T)
                    pe.wait_ge(S["wf_split"], 2 * (EX // CHUNK))
                    shared_gu(0, 0, part=0)
                    attend(b, range(0, 2))
                    shared_gu(0, 0, part=1)
                    pe.wait_ge(S["x1f_out"], KD * (NB - 2))
                    shared_gu(0, 1, part=0)
                    attend(b, range(2, TB))
                    shared_gu(0, 1, part=1)
                    o_transposed(b)
                    proj_o(b)
                    pe.wait_ge(S["sh_out"], 2)
                    x1_transposed(b - 1)
                    shared_gu(0, 2)
                if b >= 1:
                    router(b - 1)
            x1_transposed(NB - 1)
            pe.wait_ge(S["x1f_out"], KD * (NB - 1))
            shared_gu(0, 3, part=0)
            router(NB - 1)
            shared_gu(0, 3, part=1)
            shared_gu(1, 0, part=0)
            pe.wait_ge(S["lg_out"], NB)
            pe.wait_ge(S["bf_ready"], 1)
            ranks()
            shared_gu(1, 0, part=1)
            shared_gu(1, 1)
            pe.wait_ge(S["r_out"], T)
            shared_dn(0)
            for b in (1, 2):
                shared_gu(b, 2)
                shared_gu(b, 3)
                shared_gu(b + 1, 0)
                shared_gu(b + 1, 1)
                shared_dn(b)

            def e_transposed(j, u, rounds):
                pe.wait_ge(xg_in[u], 16 * rounds)
                o = bank[(4, 7)[u % 2]]
                for k in range(KD):
                    last = nc.tensor.transpose(o[:, k * P:(k + 1) * P], xg[:, u, k * P:(k + 1) * P], ident)
                last.then_inc(S["xt_e_mm"], 1)

            def experts_of(q):
                word = pe.value_load(te_i[0:1, bass.ds(q, 1)], min_val=0, max_val=(1 << (E_BITS * WORD_TILES)) - 1)
                return [(word >> (E_BITS * n)) & (NE - 1) for n in range(WORD_TILES)]

            ex_hi, ex_lo = (o[:, EX:].rearrange("p (e n) -> p e n", e=NE) for o in (wf_hi, wf_lo))

            def e_gate_up(j, u, e):
                pe.wait_ge(S["xe_lo_out"], j + 1)
                o = bank[u % 2][:, 0:2 * IM]
                for k in range(KD):
                    n = slice(k * 2 * IM, (k + 1) * 2 * IM)
                    last = split3(o, xe_hi[:, u % 2, k, :], xe_lo[:, u % 2, k, :], ex_hi[:, bass.ds(e, 1), n],
                                  ex_lo[:, bass.ds(e, 1), n], k == 0, k == KD - 1)
                last.then_inc(S["egu_mm"], 1)

            def e_h_transposed(j, u):
                pe.wait_ge(S["eh_out"], j + 1)
                nc.tensor.transpose(bank[2 + u % 2][:, 0:P], eh[:, u % 2, :], ident).then_inc(S["eht_mm"], 1)

            def e_down(j, u, e):
                pe.wait_ge(S["he_lo_out"], j + 1)
                split3(bank[5 + u % 2][:, 0:D], he_hi[:, u % 2, :], he_lo[:, u % 2, :],
                       ex_hi[:, bass.ds(e, 1), KD * 2 * IM:], ex_lo[:, bass.ds(e, 1), KD * 2 * IM:],
                       True, True).then_inc(S["ey_mm"], 1)

            pe.wait_ge(S["te_out"], 1)
            pe.wait_ge(S["wf_split"], 2 * NCH)
            expert0, expert1, expert2 = experts_of(0)[RING - 1:]
            e_transposed(0, 0, 1)
            e_transposed(1, 1, 1)
            pe.wait_ge(S["sh_out"], 3 * CS + 2)
            e_gate_up(0, 0, expert0)
            e_transposed(2, 2, 1)
            e_gate_up(1, 1, expert1)
            e_h_transposed(0, 0)
            e_transposed(3, 3, 1)
            e_gate_up(2, 2, expert2)
            e_h_transposed(1, 1)
            pe.wait_ge(S["sres_out"], 3 * TB)
            e_down(0, 0, expert0)
            for i in range(NT // RING - 1):
                experts = experts_of(i + 1)
                for v in range(RING):
                    s = i * RING + (v + 2)
                    e_transposed(s + 2, v, i + 2)
                    e_gate_up(s + 1, (v + 3) % RING, experts[v + 2])
                    e_h_transposed(s, (v + 2) % RING)
                    e_down(s - 1, (v + 1) % RING, experts[v])
            experts = experts_of(WORDS - 1)
            for s in range(NT - 2, NT + 1):
                if s + 1 < NT:
                    e_gate_up(s + 1, (s + 1) % RING, experts[s - NT + RING])
                if s < NT:
                    e_h_transposed(s, s % RING)
                e_down(s - 1, (s - 1) % RING, experts[s - NT + 2])

            pe.wait_ge(S["ey_out"], NT)
            for c in range(2, CS):
                shared_gu(3, c)
            shared_dn(3)
            for n in range(LATE, T // UNIT):
                pe.wait_ge(S["wy_out"], UNIT * (n - ALONE + 1))
                mm(shared_sums((n - LATE) * UNIT), ident, pair[n % n_pair][:, :, 1, :],
                   start=False, stop=True, skip_group_check=True).then_inc(S["sum_mm"], 1)

        @block.scalar
        def _(act):
            copy, activation = nc.scalar.copy, nc.scalar.activation
            act.wait_ge(S["b_cleared"], 2)
            copy(warm[:, 1:2], warm[:, 0:1])
            act.dma_start(b_raw[0:1, :], batt).then_inc(S["bias_in"], 16)
            act.dma_start(b_raw[32:33, :], batt).then_inc(S["bias_in"], 16)

            def split_x_hi(b):
                act.wait_ge(xt_in[b % 2], 16 * (b // 2 + 1))
                if b >= 2:
                    act.wait_ge(S["q_mm"], KD * (b - 1))
                for k in range(KD):
                    last = copy(xt_hi[:, b % 2, k, :], xt_raw[:, b % 2, k, :])
                last.then_inc(S["xhi_ready"], 1)

            def kv_out(b, t):
                act.wait_ge(S["kv_mm"], b * TB + t + 1)
                if b >= 1 and t == 0:
                    act.wait_ge(S["kvp_mm"], b)
                o = bank[t % 2]
                activation(k_sb[:, t, :], o[:, 0:D], ACT.Relu, scale=cst[:, C_DEC + t:C_DEC + t + 1])
                copy(v_sb[:, t, :, 0:P], o[:, D:2 * D].rearrange("p (k n) -> p k n", k=KD)).then_inc(S["kv_out"], 1)

            def q_out(b, ms=range(KD)):
                for m in ms:
                    act.wait_ge(S["q_mm"], KD * b + m + 1)
                    if b >= 1:
                        act.wait_ge(S["num_mm"], TB * b)
                    activation(q_t[:, m, :], bank[2 + m][:, :], ACT.Relu, bias=bq_sb[:, m:m + 1]).then_inc(S["q_out"], 1)

            def ot_hi_out(b):
                act.wait_ge(S["ot_mm"], b + 1)
                if b >= 1:
                    act.wait_ge(S["y_mm"], TB * b)
                for m in range(KD):
                    copy(ot_hi[:, m, :], bank[(4, 7)[m]][:, :]).then_inc(S["ot_hi_out"], 1)

            def x1_apply(b):
                if b == NB - 1:
                    act.wait_ge(S["nw_last_out"], 1)
                elif b == NB - 2:
                    act.wait_ge(S["nw_pool_out"], 1)
                else:
                    act.wait_ge(S["nw_out"], b + 1)
                for t in range(TB):
                    r = x1[:, b * TB + t, 0:D]
                    activation(r, r, ACT.Identity, scale=nw[:, b, 1, t:t + 1], bias=nw[:, b, 3, t:t + 1]
                               ).then_inc(S["x1_out"], 1)

            def x1f_out(b):
                act.wait_ge(S["x1t_mm"], b + 1)
                if b == 0:
                    act.wait_ge(S["zero_in"], 16 * FILLS)
                if b >= 1:
                    act.wait_ge(S["lg_mm"], b)
                    act.wait_ge(S["x1lo_out"], KD * b)
                for m in range(KD):
                    copy(x1_t[:, m, :], x1t_bank(b, m)[:, :]).then_inc(S["x1f_out"], 1)
                act.wait_ge(S["x1f_out"], KD * (b + 1))
                for m in range(KD):
                    copy(x1t_hi[:, b, m, :], x1_t[:, m, :]).then_inc(S["x1hi_out"], 1)

            def shared_sg(b, c):
                i = b * CS + c
                act.wait_ge(S["sgu_mm"], i + 1)
                if i >= 2:
                    act.wait_ge(S["sh_out"], i - 1)
                activation(sg[:, i % 2, :], bank[2 * (i % 2)][:, :], ACT.Silu).then_inc(S["sg_out"], 1)

            def shared_hh(b, c):
                i = b * CS + c
                act.wait_ge(S["sh_out"], i + 1)
                if c == 0 and b >= 1:
                    act.wait_ge(S["sdn_mm"], 2 * b)
                copy(hh_hi[:, c, :], hf[:, i % 2, :]).then_inc(S["shh_out"], 1)

            for h, (loaded, done) in enumerate(((S["xt_half_in"], S["xhi_half_out"]), (xt_in[0], S["xhi_ready"]))):
                n = slice(h * SEQ // 2, (h + 1) * SEQ // 2)
                act.wait_ge(loaded, 16)
                copy(xt_hi[:, 0, :, n], xt_raw[:, 0, :, n]).then_inc(done, 1)
            act.wait_ge(S["cst_in"], 16)
            for t in range(TB):
                kv_out(0, t)
            split_x_hi(1)
            act.wait_ge(S["small_in"], 32)
            q_out(0)
            for b in range(NB - 1):
                for t in range(TB):
                    kv_out(b + 1, t)
                if b >= 1:
                    x1_apply(b - 1)
                if b + 2 < NB:
                    split_x_hi(b + 2)
                if b == 0:
                    q_out(b + 1, [0])
                    ot_hi_out(b)
                    q_out(b + 1, [1])
                else:
                    q_out(b + 1)
                    ot_hi_out(b)
                if b >= 1:
                    x1f_out(b - 1)
            act.wait_ge(S["q_mm"], KD * NB)
            act.wait_ge(S["xlo_ready"], NB)
            shared_sg(0, 0)
            shared_sg(0, 1)
            ot_hi_out(NB - 1)
            x1_apply(NB - 2)
            shared_hh(0, 0)
            shared_hh(0, 1)
            x1f_out(NB - 2)
            shared_sg(0, 2)
            x1_apply(NB - 1)
            x1f_out(NB - 1)
            shared_hh(0, 2)
            shared_sg(0, 3)
            shared_hh(0, 3)
            shared_sg(1, 0)
            shared_sg(1, 1)
            act.wait_ge(S["gap_out"], 1)
            activation(wtmp[:, 1, :], wtmp[:, 0, :], ACT.Exp).then_inc(S["exp_out"], 1)
            for b in (1, 2):
                shared_hh(b, 0)
                shared_hh(b, 1)
                for c in (2, 3):
                    shared_sg(b, c)
                    shared_hh(b, c)
                shared_sg(b + 1, 0)
                shared_sg(b + 1, 1)

            def e_x_hi(j, u):
                act.wait_ge(S["xt_e_mm"], j + 1)
                copy(xe_hi[:, u % 2, :, :], bank[(4, 7)[u % 2]][:, 0:KD * P].rearrange("p (k n) -> p k n", k=KD)
                     ).then_inc(S["xe_hi_out"], 1)

            def e_silu(j, u):
                act.wait_ge(S["egu_mm"], j + 1)
                activation(eg[:, u % 2, :], bank[u % 2][:, 0:IM], ACT.Silu).then_inc(S["eg_out"], 1)

            def e_h_hi(j, u):
                act.wait_ge(S["eht_mm"], j + 1)
                copy(he_hi[:, u % 2, :], bank[2 + u % 2][:, 0:P]).then_inc(S["he_hi_out"], 1)

            def e_y(j, u, rounds):
                act.wait_ge(S["ey_mm"], j + 1)
                if rounds is not None:
                    act.wait_ge(ey_st[u], 16 * rounds)
                copy(ey[:, u, :], bank[5 + u % 2][:, 0:D]).then_inc(S["ey_out"], 1)

            act.wait_ge(S["y_mm"], T)
            act.wait_ge(S["lg_mm"], NB)
            act.wait_ge(S["x1lo_out"], KD * NB)
            act.wait_ge(S["num_mm"], T)
            e_x_hi(0, 0)
            e_x_hi(1, 1)
            e_silu(0, 0)
            e_x_hi(2, 2)
            e_silu(1, 1)
            e_h_hi(0, 0)
            e_x_hi(3, 3)
            e_silu(2, 2)
            e_h_hi(1, 1)
            e_y(0, 0, None)
            shared_hh(3, 0)
            shared_hh(3, 1)
            for s in range(2, 2 + RING - 1):
                e_x_hi(s + 2, (s + 2) % RING)
                e_silu(s + 1, (s + 1) % RING)
                e_h_hi(s, s % RING)
                e_y(s - 1, s - 1, None)
            with act.Fori(0, NT // RING - 2) as i:
                for v in range(RING):
                    s = i * RING + (v + RING + 1)
                    e_x_hi(s + 2, (v + 3) % RING)
                    e_silu(s + 1, (v + 2) % RING)
                    e_h_hi(s, (v + 1) % RING)
                    e_y(s - 1, v, i + 1)
            for s in range(NT - 3, NT + 1):
                if s + 2 < NT:
                    e_x_hi(s + 2, (s + 2) % RING)
                if s + 1 < NT:
                    e_silu(s + 1, (s + 1) % RING)
                if s < NT:
                    e_h_hi(s, s % RING)
                e_y(s - 1, (s - 1) % RING, (s - 1) // RING)

            def apply_norm(b, t):
                if b == NB - 1:
                    act.wait_ge(S["ln_last_out"], 1)
                else:
                    act.wait_ge(S["ln_out"], b // 2 + 1)
                r = x1[:, b * TB + t, 0:D]
                activation(r, r, ACT.Identity, scale=nw[:, b, 1, t:t + 1], bias=nw[:, b, 3, t:t + 1]
                           ).then_inc(S["fin_out"], 1)

            def weigh_second(n):
                act.wait_ge(pair_in[n], 16)
                act.wait_ge(S["wtop_out"], 1)
                for i in range(n * UNIT, (n + 1) * UNIT):
                    y = pair[n % n_pair][:, i % UNIT, 1, :]
                    activation(y, y, ACT.Identity, scale=w_top[:, 1, i:i + 1]).then_inc(S["wy_out"], 1)

            for c in range(2, CS):
                shared_sg(3, c)
                shared_hh(3, c)
            for n in range(ALONE, T // UNIT):
                weigh_second(n)
            for i in range(T - TB):
                apply_norm(i // TB, i % TB)
            for t in range(TB - LAST_ACT, TB):
                apply_norm(NB - 1, t)

        @block.vector
        def _(dve):
            v = nc.vector
            chain = [0]

            def link(*instructions):
                for ins in instructions:
                    chain[0] += 1
                    ins.then_inc(S["dve_chain"], 1)
                dve.wait_ge(S["dve_chain"], chain[0])

            def split_w(at, n):
                raw = wa_raw[:, at:at + n]
                link(v.tensor_copy(wa_hi[:, at:at + n], raw))
                return v.tensor_tensor(wa_lo[:, at:at + n], raw, wa_hi[:, at:at + n].bitcast(F32), ALU.subtract)

            v.memset(warm[:, :], 0.0).then_inc(S["b_cleared"], 1)
            v.memset(b_raw[:, :], 0.0).then_inc(S["b_cleared"], 1)
            v.memset(v_sb[:, :, :, P:P + 1], 1.0)
            link(v.memset(one_f[:, :].bitcast(F32), 0.0))
            link(v.memset(one_f[0:1, :].bitcast(F32), 1.0))
            v.memset(one_f[32:33, :].bitcast(F32), 1.0).then_inc(S["ones_ready"], 1)
            v.memset(ones[:, :], 1.0).then_inc(S["ones_ready"], 1)
            def split_first_x_lo(h, made, done):
                dve.wait_ge(made, 1)
                n = slice(h * SEQ // 2, (h + 1) * SEQ // 2)
                v.tensor_tensor(xt_lo[:, 0, :, n], xt_raw[:, 0, :, n], xt_hi[:, 0, :, n].bitcast(F32), ALU.subtract
                                ).then_inc(done, 1)

            dve.wait_ge(S["watt_in0"], 16)
            split_w(WKV, 2 * D).then_inc(S["kvw_split"], 1)
            split_first_x_lo(0, S["xhi_half_out"], S["xlo_half_out"])
            dve.wait_ge(S["watt_in0b"], 16)
            split_w(WKV + 2 * D, 2 * D).then_inc(S["kvw_split"], 1)
            split_first_x_lo(1, S["xhi_ready"], S["xlo_ready"])
            dve.wait_ge(S["bias_in"], 32)
            link(v.tensor_copy(b_row[:, :], b_raw[:, :]))
            v.tensor_tensor(b_row[32:33, :], b_raw[32:33, :], b_row[32:33, :].bitcast(F32), ALU.subtract
                            ).then_inc(S["bias_ready"], 1)
            dve.wait_ge(S["watt_in1"], 16)
            for k in range(KD):
                split_w(WQ + k * D, D).then_inc(S["qw_split"], 1)
            dve.wait_ge(S["watt_in2"], 16)
            for k in range(KD):
                split_w(WO + k * D, D).then_inc(S["ow_split"], 1)
            dve.wait_ge(S["cst_in"], 16)
            v.tensor_copy(tri[:, :], cst[:, C_TRI:C_TRI + P]).then_inc(S["bf_ready"], 1)

            def kvm_out(b):
                dve.wait_ge(S["kvp_mm"], b + 1)
                if b >= 1:
                    dve.wait_ge(S["num_mm"], TB * b)
                for m in range(KD):
                    o = bank[4][:, m * (P + 1):(m + 1) * (P + 1)]
                    v.tensor_tensor(kvm[:, m, 0:P], o[:, 0:P], blk, ALU.mult)
                    last = v.tensor_scalar(kvm[:, m, P:P + HB], headm, o[:, P:P + 1], None, ALU.mult)
                last.then_inc(S["kvm_out"], 1)

            def o_out(b, t):
                dve.wait_ge(S["num_mm"], TB * b + t + 1)
                o = bank[5 + t % 2][:, 0:KD * (P + HB)].rearrange("p (k n) -> p k n", k=KD)
                zt = z[:, t % 2]
                link(v.tensor_scalar(zt, o[:, :, P:P + HB], cst[:, C_EPS + t:C_EPS + t + 1], None, ALU.add))
                link(v.reciprocal(zt, zt))
                if t == 0 and b >= 1:
                    dve.wait_ge(S["ot_mm"], b)
                for m in range(KD):
                    last = v.tensor_tensor(
                        o_sb[:, t, m * P:(m + 1) * P].rearrange("p (h e) -> p h e", h=HB),
                        o[:, m, 0:P].rearrange("p (h e) -> p h e", h=HB),
                        zt[:, m, :].unsqueeze(2).broadcast_to([P, HB, DH]), ALU.mult)
                last.then_inc(S["o_out"], 1)

            def ot_lo_out(b):
                if b >= 1:
                    dve.wait_ge(S["y_mm"], TB * b)
                for m in range(KD):
                    dve.wait_ge(S["ot_hi_out"], KD * b + m + 1)
                    v.tensor_tensor(ot_lo[:, m, :], bank[(4, 7)[m]][:, :], ot_hi[:, m, :].bitcast(F32),
                                    ALU.subtract).then_inc(S["ot_lo_out"], 1)

            def moments(b):
                dve.wait_ge(S[f"res_in{b}"], 16)

                def stats(t):
                    dve.wait_ge(S["r_out"], TB * b + t + 1)
                    v.bn_stats(stat[:, t, :], x1[:, b * TB + t, 0:D]).then_inc(S["st_out"], 1)

                for t in range(TB):
                    dve.wait_ge(S["y_mm"], TB * b + t + 1)
                    r = x1[:, b * TB + t, 0:D]
                    v.tensor_tensor(r, bank[5 + t % 2][:, 0:D], r, ALU.add).then_inc(S["r_out"], 1)
                    if t >= 1:
                        stats(t - 1)
                stats(TB - 1)
                dve.wait_ge(S["st_out"], TB * (b + 1))
                for t in range(TB):
                    v.bn_aggr(mv[:, b, t, :], stat[:, t, :]).then_inc(S["mom_out"], 1)

            def x1_norm(b):
                dve.wait_ge(S["mom_out"], TB * (b + 1))
                rstd(v, link, slice(b, b + 1), fused=True).then_inc(S["nw_last_out" if b == NB - 1 else "nw_out"], 1)

            def top_two(b):
                dve.wait_ge(S["lg_mm"], b + 1)
                ts = slice(b * TB, (b + 1) * TB)
                v.tensor_copy(logit[:, ts, :], lg_bank.rearrange("p (t e) -> p t e", t=TB)
                              ).then_inc(S["lg_out"], 1)
                dve.wait_ge(S["lg_out"], b + 1)
                for t in range(b * TB, (b + 1) * TB):
                    link(v.max(top_v[:, t, :], logit[:, t, :]))
                    last = v.max_index(top_i[:, t, :], top_v[:, t, :], logit[:, t, :])
                link(last)

            def shared_h(b, c):
                i = b * CS + c
                dve.wait_ge(S["sg_out"], i + 1)
                if i >= 2:
                    dve.wait_ge(S["shh_out"], i - 1)
                    dve.wait_ge(S["shl_out"], i - 1)
                v.tensor_tensor(hf[:, i % 2, :], bank[2 * (i % 2) + 1][:, :], sg[:, i % 2, :], ALU.mult
                                ).then_inc(S["sh_out"], 1)

            def shared_lo(b, c):
                i = b * CS + c
                dve.wait_ge(S["shh_out"], i + 1)
                v.tensor_tensor(hh_lo[:, c, :], hf[:, i % 2, :], hh_hi[:, c, :].bitcast(F32), ALU.subtract
                                ).then_inc(S["shl_out"], 1)

            def shared_out(b):
                for t in range(TB):
                    if t % 2 == 0:
                        dve.wait_ge(S["sdn_mm"], 2 * b + t // 2 + 1)
                    r = x1[:, b * TB + t, 0:D]
                    if t == 0:
                        dve.wait_ge(S[f"scattered{b}"], 16 * TOPK * TB)
                    v.tensor_tensor(r, shared_sum(t), r, ALU.add
                                    ).then_inc(S["sres_out"], 1)

            def route():
                link(v.tensor_copy(ix_f[:, :, :], top_i[:, :, 0:TOPK]))
                v.tensor_copy(x1[:, :, D], cst[:, C_TOK:C_TOK + T]).then_inc(S["tags_out"], 1)
                v.tensor_copy(x1[:, :, D + 1], ix_f[:, :, 0]).then_inc(S["tags_out"], 1)
                iota = cst[:, C_IOTA:C_IOTA + NE].unsqueeze(1).broadcast_to([P, T, NE])
                for j in range(TOPK):
                    link(v.tensor_tensor(hot[:, j, :].rearrange("p (t e) -> p t e", t=T), iota,
                                         ix_f[:, :, j:j + 1].broadcast_to([P, T, NE]), ALU.is_equal))
                v.tensor_tensor(hot_m[:, :], hot[:, 0, :], hot[:, 1, :], ALU.add).then_inc(S["hot_out"], 1)
                v.tensor_tensor(wtmp[:, 0, :], top_v[:, :, 1], top_v[:, :, 0], ALU.subtract).then_inc(S["gap_out"], 1)

            def slots():
                c, ct = cnt, cnt_i
                dve.wait_ge(S["rank_mm"], 1)
                link(v.tensor_scalar(ct[:, 0, :], bank[4][:, T * NE:(T + 1) * NE], float(P - 1), None, ALU.add))
                link(v.tensor_scalar(ct[:, 1, :], ct[:, 0, :], P.bit_length() - 1, None, ALU.logical_shift_right))
                link(v.tensor_copy(c[:, 0, :], ct[:, 1, :]))
                link(v.memset(c[:, 1, :], 1.0))
                link(v.tensor_tensor_scan(c[:, 2, :], c[:, 1, :], c[:, 0, :], 0.0, ALU.mult, ALU.add))
                link(v.tensor_tensor(c[:, 3, :], c[:, 2, :], c[:, 0, :], ALU.subtract))
                link(v.tensor_scalar(c[:, 4, :], c[:, 3, :], float(P), None, ALU.mult))
                link(v.tensor_tensor(pos[:, :].rearrange("p (t e) -> p t e", t=T),
                                     bank[4][:, 0:T * NE].rearrange("p (t e) -> p t e", t=T),
                                     c[:, 4, :].unsqueeze(1).broadcast_to([P, T, NE]), ALU.add))
                for j in range(TOPK):
                    link(v.tensor_tensor(hot[:, j, :], hot[:, j, :], pos[:, :], ALU.mult))
                    link(v.tensor_reduce(slot_f[:, j, :], hot[:, j, :].rearrange("p (t e) -> p t e", t=T), AX.X, ALU.add))
                v.tensor_copy(slot[:, :, :], slot_f[:, :, :]).then_inc(S["slots_out"], 1)

            def tile_experts():
                c = cnt
                link(v.tensor_tensor(te_c[:, :, :], c[:, 2, :].unsqueeze(1).broadcast_to([P, NTW, NE]),
                                     cst[:, C_TILE:C_TILE + NTW].unsqueeze(2).broadcast_to([P, NTW, NE]), ALU.is_le))
                link(v.tensor_reduce(te_f[:, :], te_c[:, :, :], AX.X, ALU.add))
                link(v.tensor_scalar(te_f[:, :], te_f[:, :], float(NE - 1), None, ALU.min))
                def column(n):
                    return te_f[0:1, :].rearrange("p (q w) -> p q w", w=RING)[:, n // RING:n // RING + WORDS, n % RING]
                link(v.tensor_copy(te_w[:, :], column(WORD_TILES - 1)))
                for n in reversed(range(WORD_TILES - 1)):
                    dst = te_w if n else te_i
                    ins = v.scalar_tensor_tensor(dst[:, :], te_w[:, :], float(1 << E_BITS), column(n), ALU.mult, ALU.add)
                    if n:
                        link(ins)
                ins.then_inc(S["te_out"], 1)

            def weights():
                dve.wait_ge(S["exp_out"], 1)
                link(v.tensor_scalar(wtmp[:, 2, :], wtmp[:, 1, :], 1.0, None, ALU.add))
                link(v.reciprocal(w_top[:, 0, :], wtmp[:, 2, :]))
                v.tensor_tensor(w_top[:, 1, :], wtmp[:, 1, :], w_top[:, 0, :], ALU.mult).then_inc(S["wtop_out"], 1)
                dve.wait_ge(S["wtop_out"], 1)

            for b in range(NB - 1):
                kvm_out(b)
                for t in range(TB):
                    o_out(b, t)
                    if b >= 1 and t == 1:
                        x1_norm(b - 1)
                if b >= 2:
                    top_two(b - 2)
                ot_lo_out(b)
                moments(b)
            b = NB - 1
            kvm_out(b)
            for t in range(TB):
                o_out(b, t)
                if t == 1:
                    top_two(b - 2)
            dve.wait_ge(S["xhi_ready"], NB)
            dve.wait_ge(S["q_mm"], KD * NB)
            dve.wait_ge(S["xlo_ready"], NB)
            shared_h(0, 0)
            ot_lo_out(b)
            shared_h(0, 1)
            moments(b)
            x1_norm(b)
            top_two(b - 1)
            shared_lo(0, 0)
            shared_lo(0, 1)
            shared_h(0, 2)
            top_two(b)
            route()
            shared_h(0, 3)
            slots()
            shared_lo(0, 2)
            shared_lo(0, 3)
            tile_experts()
            shared_h(1, 0)
            shared_h(1, 1)
            weights()
            for b in (1, 2):
                shared_lo(b, 0)
                shared_lo(b, 1)
                for c in (2, 3):
                    shared_h(b, c)
                    shared_lo(b, c)
                shared_out(b - 1)
                shared_h(b + 1, 0)
                shared_h(b + 1, 1)
            shared_out(2)
            def e_x_lo(j, u):
                dve.wait_ge(S["xe_hi_out"], j + 1)
                v.tensor_tensor(xe_lo[:, u % 2, :, :],
                                bank[(4, 7)[u % 2]][:, 0:KD * P].rearrange("p (k n) -> p k n", k=KD),
                                xe_hi[:, u % 2, :, :].bitcast(F32), ALU.subtract).then_inc(S["xe_lo_out"], 1)

            def e_h(j, u):
                dve.wait_ge(S["eg_out"], j + 1)
                v.tensor_tensor(eh[:, u % 2, :], bank[u % 2][:, IM:2 * IM], eg[:, u % 2, :], ALU.mult
                                ).then_inc(S["eh_out"], 1)

            def e_h_lo(j, u):
                dve.wait_ge(S["he_hi_out"], j + 1)
                v.tensor_tensor(he_lo[:, u % 2, :], bank[2 + u % 2][:, 0:P], he_hi[:, u % 2, :].bitcast(F32),
                                ALU.subtract).then_inc(S["he_lo_out"], 1)

            def result_rows():
                dve.wait_ge(S["tag_in"], 16)
                link(v.tensor_tensor(dst_f[:, :], tag[:, :, 1], te_f[:, RING - 1:RING - 1 + NT], ALU.not_equal))
                v.tensor_tensor(dst[:, :], dst_f[:, :], tag[:, :, 0], ALU.add).then_inc(S["dst_out"], 1)

            e_x_lo(0, 0)
            e_x_lo(1, 1)
            result_rows()
            e_h(0, 0)
            e_x_lo(2, 2)
            e_h(1, 1)
            e_h_lo(0, 0)
            e_x_lo(3, 3)
            e_h(2, 2)
            e_h_lo(1, 1)
            shared_lo(3, 0)
            shared_lo(3, 1)
            with dve.Fori(0, NT // RING - 1) as i:
                for w in range(RING):
                    s = i * RING + (w + 2)
                    e_x_lo(s + 2, w)
                    e_h(s + 1, (w + 3) % RING)
                    e_h_lo(s, (w + 2) % RING)
            e_h(NT - 1, (NT - 1) % RING)
            for s in (NT - 2, NT - 1):
                e_h_lo(s, s % RING)

            def combine(n):
                dve.wait_ge(pair_in[n], 16)
                tiles = range(n * UNIT, (n + 1) * UNIT)
                rest = [x1[:, i, 0:D] for i in tiles]
                y = pair[n % n_pair]
                if n >= LATE:
                    dve.wait_ge(S["sum_mm"], n - LATE + 1)
                    dve.wait_ge(S[f"scattered{NB - 1}"], 16 * TOPK * TB)
                    rest = [shared_sum(i % TB) for i in tiles]
                elif n < ALONE:
                    dve.wait_ge(S["sres_out"], tiles[-1] + 1)
                    link(*[v.scalar_tensor_tensor(x1[:, i, 0:D], y[:, i % UNIT, 1, :], w_top[:, 1, i:i + 1],
                                                  x1[:, i, 0:D], ALU.mult, ALU.add) for i in tiles])
                else:
                    dve.wait_ge(S["add_out"], UNIT * (n - ALONE + 1))
                for i in tiles:
                    v.scalar_tensor_tensor(x1[:, i, 0:D], y[:, i % UNIT, 0, :], w_top[:, 0, i:i + 1],
                                           rest[i % UNIT], ALU.mult, ALU.add).then_inc(S["acc_out"], 1)
                for i in tiles:
                    dve.wait_ge(S["acc_out"], i + 1)
                    ins = v.bn_stats(stat[:, i % TB, :], x1[:, i, 0:D])
                    if i == tiles[-1]:
                        link(ins)
                    else:
                        ins.then_inc(S["stat_out"], 1)
                dve.wait_ge(S["stat_out"], n + 1)
                b = tiles[0] // TB
                for i in tiles:
                    v.bn_aggr(mv[:, b, i % TB, :], stat[:, i % TB, :]).then_inc(S["bn_out"], 1)

            def apply_norm(b, t):
                r = x1[:, b * TB + t, 0:D]
                v.tensor_scalar(r, r, nw[:, b, 1, t:t + 1], nw[:, b, 3, t:t + 1], ALU.mult, ALU.add
                                ).then_inc(S["fin_last_out"], 1)

            for c in range(2, CS):
                shared_h(3, c)
                shared_lo(3, c)
            for n in range(T // UNIT):
                combine(n)
            dve.wait_ge(S["bn_out"], T)
            rstd(v, link, slice(NB - 1, NB), fused=True).then_inc(S["ln_last_out"], 1)
            dve.wait_ge(S["ln_last_out"], 1)
            for t in range(TB - LAST_ACT):
                apply_norm(NB - 1, t)

        @block.gpsimd
        def _(pool):
            g = nc.gpsimd
            g.memset(fill[:, 0:D], 0.0).then_inc(S["pool_chain"], 1)
            pool.wait_ge(S["cst_in"], 16)
            g.tensor_copy(fill[:, D:DT], cst[:, C_FILL:C_FILL + TAG]).then_inc(S["pool_chain"], 1)
            pool.wait_ge(S["pool_chain"], 2)
            pool.sem_inc(S["fill_made"], 1)

            chain = [2]

            def link(ins):
                chain[0] += 1
                ins.then_inc(S["pool_chain"], 1)
                pool.wait_ge(S["pool_chain"], chain[0])

            def split_x_lo(b):
                pool.wait_ge(S["xhi_ready"], b + 1)
                for k in range(KD):
                    last = g.tensor_tensor(xt_lo[:, b % 2, k, :], xt_raw[:, b % 2, k, :],
                                           xt_hi[:, b % 2, k, :].bitcast(F32), ALU.subtract)
                last.then_inc(S["xlo_ready"], 1)

            def split_chunk(i):
                pool.wait_ge(stage_in[i % 2], 16 * (i // 2 + 1))
                c = slice(i * CHUNK, (i + 1) * CHUNK)
                g.tensor_copy(wf_hi[:, c], stage[:, i % 2, :]).then_inc(S["wf_split"], 1)
                pool.wait_ge(S["wf_split"], 2 * i + 1)
                g.tensor_tensor(wf_lo[:, c], stage[:, i % 2, :], wf_hi[:, c].bitcast(F32), ALU.subtract
                                ).then_inc(S["wf_split"], 1)

            def x1_lo(b):
                pool.wait_ge(S["x1hi_out"], KD * (b + 1))
                for m in range(KD):
                    g.tensor_tensor(x1t_lo[:, b, m, :], x1_t[:, m, :], x1t_hi[:, b, m, :].bitcast(F32),
                                    ALU.subtract).then_inc(S["x1lo_out"], 1)

            per = -(-NCH // NB)
            split_x_lo(1)
            done = 0
            for b in range(NB):
                for n in range(per):
                    if done < NCH:
                        split_chunk(done)
                        done += 1
                    if n == 1 and b + 2 < NB:
                        split_x_lo(b + 2)
                    if n == 3 and b >= 1 and b < NB - 1:
                        x1_lo(b - 1)
                    if n == 0 and b == NB - 1:
                        pool.wait_ge(S["mom_out"], TB * b)
                        rstd(g, link, slice(b - 1, b), fused=False).then_inc(S["nw_pool_out"], 1)
            x1_lo(NB - 2)
            x1_lo(NB - 1)

            pool.wait_ge(S["zero_in"], 16 * FILLS)
            pool.wait_ge(S["slots_out"], 1)
            pool.wait_ge(S["tags_out"], 2)
            pool.wait_ge(S["x1_out"], T)
            for t in range(T):
                for j in range(TOPK):
                    pool.indirect_dma_start(out=x_scat, out_offset=bass.IndirectOffsetOnAxis(ap=slot[:, j, t:t + 1], axis=0),
                                            in_=x1[:, t, :], in_offset=None).then_inc(S[f"scattered{t // TB}"], 16)
            def send(j, u):
                pool.wait_ge(S["ey_out"], j + 1)
                pool.indirect_dma_start(out=y_scat, out_offset=bass.IndirectOffsetOnAxis(ap=dst[:, j:j + 1], axis=0),
                                        in_=ey[:, u, :], in_offset=None,
                                        bounds_check=2 * TOK - 1, oob_is_err=False).then_inc(ey_st[u], 16)

            pool.wait_ge(S["dst_out"], 1)
            for j in range(NT):
                send(j, j % RING)

            def add_second(n):
                pool.wait_ge(S["wy_out"], UNIT * (n - ALONE + 1))
                pool.wait_ge(S["sres_out"], UNIT * (n + 1))
                for i in range(n * UNIT, (n + 1) * UNIT):
                    g.tensor_tensor(x1[:, i, 0:D], pair[n % n_pair][:, i % UNIT, 1, :], x1[:, i, 0:D], ALU.add
                                    ).then_inc(S["add_out"], 1)

            for n in range(ALONE, LATE):
                add_second(n)
            pool.wait_ge(S["bn_out"], 2 * TB)
            rstd(g, link, slice(0, 2), fused=False).then_inc(S["ln_out"], 1)
            pool.wait_ge(S["bn_out"], 3 * TB)
            rstd(g, link, slice(2, 3), fused=False).then_inc(S["ln_out"], 1)


def constants():
    p = np.arange(P)
    c = np.zeros((P, NC_), np.float32)
    c[:, C_ID:C_ID + P] = np.eye(P)
    c[:, C_BLK:C_BLK + P] = p[:, None] // DH == p[None, :] // DH
    c[:, C_HEAD:C_HEAD + HB] = p[:, None] // DH == np.arange(HB)[None, :]
    decay = np.exp(-(np.arange(TB)[None, :] * P + p[:, None]).astype(np.float32) / np.float32(SEQ))
    c[:, C_DEC:C_DEC + TB] = decay
    c[:, C_EPS:C_EPS + TB] = np.float32(EPS_ATT) / decay
    c[:, C_IOTA:C_IOTA + NE] = np.arange(NE)
    c[:, C_TRI:C_TRI + P] = p[:, None] < p[None, :]
    c[:, C_TILE:C_TILE + NTW] = np.arange(NTW) - (RING - 1)
    c[:, C_TOK:C_TOK + T] = 2 * (np.arange(T)[None, :] * P + p[:, None])
    c[:, C_FILL:C_FILL + TAG] = np.stack([2 * (TOK + p), -np.ones(P)], axis=1)
    return c


def rows(w):
    return w.reshape(-1, P, w.shape[-1]).transpose(1, 0, 2).reshape(P, -1)


def kernel(**inputs):
    import concourse.bacc as bacc
    from concourse.bass_utils import run_bass_kernel_spmd

    a = {n.replace("L0_", ""): np.asarray(v) for n, v in inputs.items()}
    x = a["attn_x"]
    wkv = np.concatenate([a["attn_Wk"].T, a["attn_Wv"].T], axis=1)
    gu, dn = a["ffn_w_gate_up"], a["ffn_w_down"]
    arrays = {
        "xT": np.stack([rows(x[b].T) for b in range(NB)]),
        "x": x,
        "watt": np.concatenate([rows(wkv), rows(a["attn_Wq"].T), rows(a["attn_Wo"].T)], axis=1),
        "batt": np.concatenate([a["attn_bk"], a["attn_bv"], a["attn_bo"]])[None, :],
        "bq": rows(a["attn_bq"][:, None]),
        "wffn": np.concatenate([rows(a["ffn_w_sh_gate_up"]), rows(a["ffn_w_sh_down"])]
                               + [rows(w[e]) for e in range(NE) for w in (gu, dn)], axis=1),
        "wgate": rows(a["ffn_w_gate"]).reshape(P, KD, NE),
        "consts": constants(),
    }
    arrays = {n: np.ascontiguousarray(v) for n, v in arrays.items()}
    nc = bacc.Bacc("TRN2", target_bir_lowering=False, num_devices=1)
    aps = [nc.dram_tensor(f"in_{n}", v.shape, mybir.dt.from_np(v.dtype), kind="ExternalInput").ap()
           for n, v in arrays.items()]
    out = nc.dram_tensor("out_0", [NB, SEQ, D], F32, kind="ExternalOutput").ap()
    build(nc, *aps, out)
    r = run_bass_kernel_spmd(nc, [{f"in_{n}": v for n, v in arrays.items()}], core_ids=[0])
    return r.results[0]["out_0"]
```
